# Optimizing a Trainium2 kernel written in Bass

```python
import numpy as np
import jax
import jax.numpy as jnp

def _softmax(x, axis=-1):
    return jax.nn.softmax(x, axis=axis)

def _gelu(x):
    return jax.nn.gelu(x, approximate=True)

def _silu(x):
    return jax.nn.silu(x)

def _sigmoid(x):
    return jax.nn.sigmoid(x)

def _layernorm(x, axis=-1, eps=1e-05):
    m = jnp.mean(x, axis=axis, keepdims=True)
    v = jnp.var(x, axis=axis, keepdims=True)
    return (x - m) / jnp.sqrt(v + eps)

def _scatter_add(tgt, idx, src, axis=0):
    return tgt.at[idx].add(src)

def _segment_sum(src, seg, n):
    return jax.ops.segment_sum(src, seg, n)
kernel_name = 'mk_recurrent_d1_jaxref_r8_216fce'

def setup_inputs(seed: int=0):
    np.random.seed(seed)
    _w = jnp.asarray

    def _L0_attn_setup():
        import jax, jax.numpy as jnp
        import numpy as np
        B, T, C, H = (2, 256, 256, 16)
        HD = C // H
        BASE = 10000.0

        def _rope_tables(seq_len, d):
            p = jnp.arange(d // 2, dtype=jnp.float32)
            theta = jnp.power(BASE, -2.0 ** p / d)
            pos = jnp.arange(1, seq_len + 1, dtype=jnp.float32)[:, None]
            c = pos * theta
            ang = jnp.concatenate([c, c], axis=-1)
            return (jnp.cos(ang), jnp.sin(ang))

        def _rope(x):
            d = x.shape[-1]
            cos, sin = _rope_tables(x.shape[-2], d)
            half = d // 2
            x_rot = jnp.concatenate([-x[..., half:], x[..., :half]], axis=-1)
            return x * cos + x_rot * sin
        key = jax.random.key(seed)
        k1, k2, k3 = jax.random.split(key, 3)
        x = jax.random.normal(k1, (B, T, C), dtype=jnp.float32)
        Wqkv = jax.random.normal(k2, (3 * C, C), dtype=jnp.float32) * 0.02
        bqkv = jnp.zeros((3 * C,), dtype=jnp.float32)
        Wo = jax.random.normal(k3, (C, C), dtype=jnp.float32) * 0.02
        bo = jnp.zeros((C,), dtype=jnp.float32)
        return {'x': x, 'Wqkv': Wqkv, 'bqkv': bqkv, 'Wo': Wo, 'bo': bo}
    _L0_attn_in = _L0_attn_setup()

    def _L0_ffn_setup():
        import math
        import jax, jax.numpy as jnp
        import numpy as np
        DIM = 256
        RANK = 8
        B, T = (4, 512)

        def _orthogonal(key, n):
            a = jax.random.normal(key, (n, n), dtype=jnp.float32)
            q, r = jnp.linalg.qr(a)
            q = q * jnp.sign(jnp.diagonal(r))[None, :]
            return q
        key = jax.random.key(seed)
        kx, kf = jax.random.split(key)
        x = jax.random.normal(kx, (B, T, DIM), dtype=jnp.float32)
        fkeys = jax.random.split(kf, RANK)
        factors = jnp.stack([_orthogonal(fkeys[r], DIM) * (r + 1) ** (-0.5) for r in range(RANK)])
        bias = jnp.zeros((DIM,), dtype=jnp.float32)
        return {'x': x, 'factors': factors, 'bias': bias}
    _L0_ffn_in = _L0_ffn_setup()
    _d = {'L0_attn_x': _L0_attn_in['x'], 'L0_attn_Wqkv': _L0_attn_in['Wqkv'], 'L0_attn_bqkv': _L0_attn_in['bqkv'], 'L0_attn_Wo': _L0_attn_in['Wo'], 'L0_attn_bo': _L0_attn_in['bo'], 'L0_ffn_factors': _L0_ffn_in['factors'], 'L0_ffn_bias': _L0_ffn_in['bias']}
    _x0 = _d['L0_attn_x']
    _d['L0_attn_x'] = jax.random.normal(jax.random.fold_in(jax.random.key(seed), 1), (4, 512, 256), dtype=_x0.dtype)
    del _x0
    return _d

def reference(L0_attn_x, L0_attn_Wqkv, L0_attn_bqkv, L0_attn_Wo, L0_attn_bo, L0_ffn_factors, L0_ffn_bias):

    def _L0_attn_ref(x, Wqkv, bqkv, Wo, bo):
        import jax, jax.numpy as jnp
        import numpy as np
        B, T, C, H = (2, 256, 256, 16)
        HD = C // H
        BASE = 10000.0

        def _rope_tables(seq_len, d):
            p = jnp.arange(d // 2, dtype=jnp.float32)
            theta = jnp.power(BASE, -2.0 ** p / d)
            pos = jnp.arange(1, seq_len + 1, dtype=jnp.float32)[:, None]
            c = pos * theta
            ang = jnp.concatenate([c, c], axis=-1)
            return (jnp.cos(ang), jnp.sin(ang))

        def _rope(x):
            d = x.shape[-1]
            cos, sin = _rope_tables(x.shape[-2], d)
            half = d // 2
            x_rot = jnp.concatenate([-x[..., half:], x[..., :half]], axis=-1)
            return x * cos + x_rot * sin
        b, t, c = x.shape
        qkv = x @ Wqkv.T + bqkv
        q, k, v = jnp.split(qkv, 3, axis=-1)

        def to_heads(z):
            return z.reshape(b, t, H, HD).transpose(0, 2, 1, 3)
        q, k, v = (to_heads(q), to_heads(k), to_heads(v))
        q = _rope(q)
        k = _rope(k)
        scale = 1.0 / jnp.sqrt(jnp.float32(HD))
        att = jnp.einsum('bhqd,bhkd->bhqk', q, k) * scale
        causal = jnp.tril(jnp.ones((t, t), dtype=bool))
        att = jnp.where(causal, att, -jnp.inf)
        att = jax.nn.softmax(att, axis=-1)
        y = jnp.einsum('bhqk,bhkd->bhqd', att, v)
        y = y.transpose(0, 2, 1, 3).reshape(b, t, c)
        y = y @ Wo.T + bo
        return y

    def _L0_ffn_ref(x, factors, bias):
        import math
        import jax, jax.numpy as jnp
        import numpy as np
        DIM = 256
        RANK = 8
        B, T = (4, 512)

        def _orthogonal(key, n):
            a = jax.random.normal(key, (n, n), dtype=jnp.float32)
            q, r = jnp.linalg.qr(a)
            q = q * jnp.sign(jnp.diagonal(r))[None, :]
            return q
        rank = factors.shape[0]
        mixed = jnp.einsum('btd,rde->bte', x, factors)
        mixed = mixed / math.sqrt(rank) + bias
        return mixed
    x = L0_attn_x
    xn = _layernorm(x, axis=-1)
    s = _L0_attn_ref(xn, L0_attn_Wqkv, L0_attn_bqkv, L0_attn_Wo, L0_attn_bo)
    g = _silu(_L0_ffn_ref(xn, L0_ffn_factors, L0_ffn_bias))
    x = x + s * g
    return x

_drawn_inputs = setup_inputs


def setup_inputs(seed=0):
    import zlib

    import numpy as np

    out = dict(_drawn_inputs(seed))
    spreads = {'L0_attn_bqkv': (0.0, 0.754), 'L0_attn_bo': (0.0, 0.397), 'L0_ffn_bias': (0.0, 0.8)}
    factors = {'L0_attn_Wqkv': 8.0, 'L0_attn_Wo': 4.974}
    for name, (base, spread) in spreads.items():
        noise = np.random.default_rng([zlib.crc32(name.encode()), seed]).standard_normal(out[name].shape)
        drawn = base * np.exp(spread * noise) if base else spread * noise
        out[name] = jnp.asarray(drawn.astype(out[name].dtype))
    for name, factor in factors.items():
        out[name] = (out[name] * factor).astype(out[name].dtype)
    return out
```

```python
from contextlib import ExitStack

import numpy as np

import concourse.bass as bass
from concourse import mybir

ALU = mybir.AluOpType
ACT = mybir.ActivationFunctionType
AX_X = mybir.AxisListType.X
F32 = mybir.dt.float32
BF16 = mybir.dt.bfloat16

P = 128
B, T, C = 4, 512, 256
H, HD = 16, 16
HALF = HD // 2
RANK = 8
QT = T // P
KC = C // P
GROUPS = H // 4
PAIRS = H // 2
EPS = 1e-5
MASKED = -1e30

Q_PARTS = (0, 0, 1, 1, 0, 2)
K_PARTS = (0, 1, 0, 1, 2, 0)
DOT_ROWS = len(Q_PARTS) * HD
SHIFT_ROWS = 2
ROWS = DOT_ROWS + SHIFT_ROWS

SCORE_BANKS = 3
EXP_BANKS = 2
WORK_BANKS = 2
X_SLOTS = 3
PROB_SLOTS = 4

MAX_CHUNKS = 11
EXP_CHUNKS = 5


def max_chunk(group, c):
    h = 4 * group
    if c < 4:
        return 3, [h + c]
    if c < 8:
        return 2, [h + c - 4]
    if c < 10:
        return 1, [h + 2 * (c - 8), h + 2 * (c - 8) + 1]
    return 0, [h, h + 1, h + 2, h + 3]


def exp_chunk(pair, c):
    h = 2 * pair
    if c < 2:
        return [(h + c, 0, 0)]
    if c < 4:
        return [(h + c - 2, 1, 0), (h + c - 2, 3, 3 * P)]
    return [(h, 2, 0), (h + 1, 2, 2 * P)]


def prob_place(head, key_tile):
    for c in range(EXP_CHUNKS):
        for h, j, col in exp_chunk(head // 2, c):
            if (h, j) == (head, key_tile):
                return c, col


def projection_steps(b):
    s = [("normalise", b, 0), ("turn_x", b, 0), ("turn_x", b, 1)]
    s += [("project_qk", b, 0), ("project_qk", b, 1), ("rotate", b, 0), ("high", b, 0),
          ("project_qk", b, 2), ("project_qk", b, 3), ("rest", b, 0), ("middle", b, 0),
          ("rotate", b, 1), ("high", b, 1), ("low", b, 0), ("rest", b, 1), ("middle", b, 1),
          ("low", b, 1)]
    return s


def value_steps(b):
    return [("project_vg", b, t) for t in range(QT)] + [("gate_exp", b, 0), ("gate", b, 0)]


def stack_steps(b):
    return [("stack", b, 0), ("stack", b, 1)]


def max_steps(b):
    return [("maxima", b, i) for i in range(GROUPS * MAX_CHUNKS)] + [("shift", b, 0)]


def attention_steps(b):
    s = []
    for pair in range(PAIRS):
        for c in range(EXP_CHUNKS):
            s.append(("scores", b, pair * EXP_CHUNKS + c))
            g = pair // 2 - 1
            if pair % 2 == 0 and g >= 0:
                if c == 1:
                    s.append(("values", b, g))
                if c == 3:
                    s.append(("take_o", b, g))
            if pair % 2 == 1 and g >= 0 and c == 0:
                s.append(("turn_o", b, g))
    g = GROUPS - 1
    return s + [("values", b, g), ("take_o", b, g), ("turn_o", b, g)]


def output_steps(b):
    return [("turn_y", b, 0), ("turn_y", b, 1), ("project_o", b, 0), ("project_o", b, 1)]


def merge(main, side, share):
    out, k = [], 0
    for i, step in enumerate(main):
        out.append(step)
        want = min(len(side), int(np.ceil(len(side) * (i + 1) / (len(main) * share))))
        out += side[k:want]
        k = max(k, want)
    return out + side[k:]


def plan():
    steps = [("load", 0, 0), ("load", 1, 0)] + projection_steps(0) + stack_steps(0)
    steps += value_steps(0) + projection_steps(1)
    steps += max_steps(0) + stack_steps(1)
    for b in range(B):
        side = output_steps(b - 1) if b else []
        if b + 1 < B:
            side += value_steps(b + 1)
        if b + 2 < B:
            side += [("load", b + 2, 0)] + projection_steps(b + 2)
        if b + 1 < B:
            side += max_steps(b + 1)
        steps += merge(attention_steps(b), side, 0.93)
        if b + 2 < B:
            steps += stack_steps(b + 2)
    return steps + output_steps(B - 1)


WORK_KINDS = ("turn_x", "project_qk", "project_vg", "shift", "turn_o", "turn_y", "project_o")


def block_kernel(nc, x, wqk, bqk, wv, wo, factors, bias_rows, cos, sin, out):
    steps = plan()
    seen, nth, work_order = {}, {}, []
    for step in steps:
        seen[step[0]] = seen.get(step[0], 0) + 1
        nth[step] = seen[step[0]]
        if step[0] in WORK_KINDS:
            work_order.append(step)
    work_use = {step: n for n, step in enumerate(work_order)}

    def count(kind, b, i=0):
        return nth[(kind, b, i)]

    with ExitStack() as ctx:
        def sb(name, shape, dt=F32):
            return ctx.enter_context(nc.sbuf_tensor(name, shape, dt))

        def bank(name):
            return ctx.enter_context(nc.psum_tensor(name, [P, 512], F32))

        def sem(name):
            return ctx.enter_context(nc.semaphore(name))

        ident = sb("ident", [P, P])
        ident_bf = sb("ident_bf", [P, P], BF16)
        later_k = sb("later_k", [P, P], BF16)
        later_q = sb("later_q", [P, P], BF16)
        cos_t = sb("cos_t", [P, T])
        sin_t = sb("sin_t", [P, T])
        wqk_sb = sb("wqk_sb", [P, KC, 4 * P])
        bqk_sb = sb("bqk_sb", [P, 4])
        wvg_sb = sb("wvg_sb", [P, KC, 2 * C])
        wo_sb = sb("wo_sb", [P, KC, C])
        bias_sb = sb("bias_sb", [P, 3 * C])
        xbuf = sb("xbuf", [P, X_SLOTS, QT, C])
        stats = sb("stats", [P, QT, 6])
        moments = sb("moments", [P, QT, 2])
        rstd = sb("rstd", [P, QT])
        minus_half = sb("minus_half", [P, QT])
        xn = sb("xn", [P, QT, C])
        xnT = sb("xnT", [P, KC, T])
        by_cos = sb("by_cos", [P, 2, T])
        by_sin = sb("by_sin", [P, 2, T])
        rotated = sb("rotated", [P, 2, 2, T])
        parts = sb("parts", [P, 2, 3, 2, T], BF16)
        qk = [[sb(f"stack_{n}{i}", [P, H, T], BF16) for n in "qk"] for i in range(2)]
        vaug = sb("vaug", [P, 2, QT, H, HD + 1])
        gate = sb("gate", [P, 2, QT, C])
        gate_e = sb("gate_e", [P, QT, C])
        rowmax = sb("rowmax", [P, QT, H])
        shift = sb("shift", [H, SHIFT_ROWS, T], BF16)
        probs = sb("probs", [P, PROB_SLOTS, EXP_CHUNKS, T])
        oT = sb("oT", [P, T])
        rden = sb("rden", [P, QT, 4])
        y = sb("y", [P, QT, C])
        yT = sb("yT", [P, KC, T])
        result = sb("result", [P, 2, 2, C])
        fac = probs[:, 0:2, :, :].rearrange("p a c t -> p (a c t)")[:, 0:KC * RANK * C].rearrange(
            "p (k r e) -> p k r e", k=KC, r=RANK)

        score_ps = [bank(f"score_ps{i}") for i in range(SCORE_BANKS)]
        exp_ps = [bank(f"exp_ps{i}") for i in range(EXP_BANKS)]
        o_ps = bank("o_ps")
        work_ps = [bank(f"work_ps{i}") for i in range(WORK_BANKS)]

        s_weights = sem("weights_loaded")
        s_vweights = sem("vg_weights_loaded")
        s_x = [sem(f"x_loaded{i}") for i in range(X_SLOTS)]
        s_consts = sem("constants_built")
        s_pool_own = sem("pool_own")
        s_dve_own = sem("dve_own")
        s_ones = sem("ones_set")
        s_factors = sem("factors_summed")
        done_pe = {k: sem(f"pe_{k}") for k in WORK_KINDS + ("maxima", "scores", "values")}
        taken = {k: sem(f"taken_{k}") for k in WORK_KINDS + ("maxima", "scores", "take_o")}
        s_moments = sem("moments_ready")
        s_xn = sem("xn_ready")
        s_rotated = sem("rotated_ready")
        s_high = sem("high_ready")
        s_rest = sem("rest_ready")
        s_middle = sem("middle_ready")
        s_low = sem("low_ready")
        s_stack = [[sem(f"stacked_{n}{i}") for n in "qk"] for i in range(2)]
        s_shift = [sem(f"shift_stacked{i}") for i in range(2)]
        s_gate_e = sem("gate_exp_ready")
        s_gate = sem("gate_ready")
        s_gated = sem("output_gated")
        s_result = sem("result_ready")
        s_out = [sem(f"out_stored{i}") for i in range(2)]

        x_v = x.rearrange("b (t p) c -> b p t c", p=P)
        out_v = out.rearrange("b (t p) c -> b p t c", p=P)

        def work(step):
            return work_ps[work_use[step] % WORK_BANKS]

        def wait_work_bank(pe, step):
            n = work_use[step] - WORK_BANKS
            if n >= 0:
                before = work_order[n]
                pe.wait_ge(taken[before[0]], nth[before])

        block = ctx.enter_context(nc.Block())

        @block.sync
        def _(sp):
            sp.dma_start(xbuf[:, 0], x_v[0]).then_inc(s_x[0], 16)
            sp.dma_start(wqk_sb[:], wqk.rearrange("(k p) n -> p k n", p=P)).then_inc(s_weights, 16)
            sp.dma_start(bqk_sb[:], bqk).then_inc(s_weights, 16)
            sp.dma_start(cos_t[:], cos).then_inc(s_weights, 16)
            sp.dma_start(sin_t[:], sin).then_inc(s_weights, 16)
            for k in range(KC):
                sp.dma_start(fac[:, k], factors[:, k * P:(k + 1) * P, :].rearrange("r p e -> p r e")
                             ).then_inc(s_vweights, 16)
            sp.dma_start(wvg_sb[:, :, 0:C], wv.rearrange("(k p) n -> p k n", p=P)).then_inc(s_vweights, 16)
            sp.dma_start(bias_sb[:], bias_rows).then_inc(s_vweights, 16)
            sp.dma_start(wo_sb[:], wo.rearrange("(k p) n -> p k n", p=P)).then_inc(s_vweights, 16)
            for kind, b, i in steps:
                if kind == "load" and b > 0:
                    if b >= X_SLOTS:
                        sp.wait_ge(s_result, count("project_o", b - X_SLOTS, 1))
                    sp.dma_start(xbuf[:, b % X_SLOTS], x_v[b]).then_inc(s_x[b % X_SLOTS], 16)
                elif kind == "stack":
                    sp.wait_ge(s_low, count("low", b, i))
                    sp.wait_ge(s_middle, count("middle", b, i))
                    if b >= 2:
                        sp.wait_ge(done_pe["scores"], (b - 1) * PAIRS * EXP_CHUNKS)
                    for g, part in enumerate((Q_PARTS, K_PARTS)[i]):
                        for half in range(2):
                            row = g * HD + half * HALF
                            sp.dma_start(qk[b % 2][i][row:row + HALF, :, :],
                                         parts[:, i, part, half, :]).then_inc(s_stack[b % 2][i], 16)
                elif kind == "shift":
                    sp.wait_ge(taken["shift"], count("shift", b))
                    for r in range(SHIFT_ROWS):
                        sp.dma_start(qk[b % 2][0][DOT_ROWS + r:DOT_ROWS + r + 1, :, :],
                                     shift[:, r, :]).then_inc(s_shift[b % 2], 16)
                elif kind == "project_o":
                    n = count(kind, b, i)
                    sp.wait_ge(s_result, n)
                    sp.dma_start(out_v[b, :, 2 * i:2 * i + 2, :], result[:, i]).then_inc(s_out[i], 16)
            for i in range(2):
                sp.wait_ge(s_out[i], 16 * B)

        @block.tensor
        def _(pe):
            for step in steps:
                kind, b, i = step
                if kind in WORK_KINDS:
                    wait_work_bank(pe, step)
                    ps = work(step)
                if kind == "turn_x":
                    if b == 0 and i == 0:
                        pe.wait_ge(s_consts, 4)
                    pe.wait_ge(s_xn, count("normalise", b))
                    for t in range(QT):
                        mm = pe.transpose(ps[:, t * P:(t + 1) * P], xn[:, t, i * P:(i + 1) * P], ident[:])
                    mm.then_inc(done_pe[kind], 1)
                elif kind == "project_qk":
                    if b == 0 and i == 0:
                        pe.wait_ge(s_weights, 64)
                    pe.wait_ge(taken["turn_x"], count("turn_x", b, KC - 1))
                    for k in range(KC):
                        mm = pe.matmul(ps[:, :], wqk_sb[:, k, i * P:(i + 1) * P], xnT[:, k, :],
                                       start=(k == 0), stop=(k == KC - 1))
                    mm.then_inc(done_pe[kind], 1)
                elif kind == "project_vg":
                    if b == 0 and i == 0:
                        pe.wait_ge(s_vweights, 80)
                        pe.wait_ge(s_factors, 1)
                    for k in range(KC):
                        mm = pe.matmul(ps[:, :], xnT[:, k, i * P:(i + 1) * P], wvg_sb[:, k, :],
                                       start=(k == 0), stop=(k == KC - 1))
                    mm.then_inc(done_pe[kind], 1)
                elif kind == "maxima":
                    n = count(kind, b, i)
                    if n > SCORE_BANKS:
                        pe.wait_ge(taken[kind], n - SCORE_BANKS)
                    if i == 0:
                        for s in range(2):
                            pe.wait_ge(s_stack[b % 2][s], 16 * 12 * (b // 2 + 1))
                    sps = score_ps[(n - 1) % SCORE_BANKS]
                    tile, heads = max_chunk(i // MAX_CHUNKS, i % MAX_CHUNKS)
                    width = (tile + 1) * P
                    for s, h in enumerate(heads):
                        pe.matmul(sps[:, s * width:(s + 1) * width],
                                  qk[b % 2][0][0:DOT_ROWS, h, tile * P:(tile + 1) * P],
                                  qk[b % 2][1][0:DOT_ROWS, h, 0:width], start=(s == 0), stop=False)
                    diagonal = sps[:, 0:len(heads) * width].rearrange("p (h k) -> p h k", k=width)[:, :, tile * P:]
                    mm = pe.matmul(diagonal, ident_bf[:], later_k[:].unsqueeze(1).broadcast_to([P, len(heads), P]), start=False, stop=True)
                    mm.then_inc(done_pe[kind], 1)
                elif kind == "shift":
                    pe.wait_ge(taken["maxima"], count("maxima", b, GROUPS * MAX_CHUNKS - 1))
                    for t in range(QT):
                        mm = pe.transpose(ps[0:H, t * P:(t + 1) * P], rowmax[:, t, :], ident[:])
                    mm.then_inc(done_pe[kind], 1)
                elif kind == "scores":
                    n = count(kind, b, i)
                    if n > EXP_BANKS:
                        pe.wait_ge(taken[kind], n - EXP_BANKS)
                    if i == 0:
                        pe.wait_ge(s_shift[b % 2], 16 * SHIFT_ROWS * (b // 2 + 1))
                        if b == 0:
                            pe.wait_ge(s_ones, 3)
                    eps = exp_ps[(n - 1) % EXP_BANKS]
                    blocks = exp_chunk(i // EXP_CHUNKS, i % EXP_CHUNKS)
                    for n, (h, j, col) in enumerate(blocks):
                        pe.matmul(eps[:, col:col + T - j * P],
                                  qk[b % 2][1][0:ROWS, h, j * P:(j + 1) * P],
                                  qk[b % 2][0][0:ROWS, h, j * P:T], start=(n == 0), stop=False)
                    if len(blocks) == 1:
                        diagonal = eps[:, 0:P]
                    else:
                        step_c = blocks[1][2] // P
                        diagonal = eps[:, :].rearrange("p (n q) -> p n q", q=P)[:, 0:step_c + 1:step_c, :]
                    mm = pe.matmul(diagonal, ident_bf[:], later_q[:].unsqueeze(1).broadcast_to([P, len(blocks), P]), start=False, stop=True)
                    mm.then_inc(done_pe[kind], 1)
                elif kind == "values":
                    pe.wait_ge(taken["scores"], (b * PAIRS + 2 * i + 2) * EXP_CHUNKS)
                    n = count(kind, b, i)
                    if n > 1:
                        pe.wait_ge(taken["take_o"], n - 1)
                    if i == 0:
                        pe.wait_ge(taken["project_vg"], count("project_vg", b, QT - 1))
                    for j in range(QT):
                        for s in range(4):
                            h = 4 * i + s
                            c, col = prob_place(h, j)
                            slot = (b * PAIRS + h // 2) % PROB_SLOTS
                            mm = pe.matmul(o_ps[32 * s:32 * s + HD + 1, j * P:T], vaug[:, b % 2, j, h, :],
                                           probs[:, slot, c, col:col + T - j * P],
                                           start=(j == 0), stop=(j == QT - 1))
                    mm.then_inc(done_pe[kind], 1)
                elif kind == "turn_o":
                    pe.wait_ge(taken["take_o"], count("take_o", b, i))
                    for t in range(QT):
                        mm = pe.transpose(ps[:, t * P:(t + 1) * P], oT[:, t * P:(t + 1) * P], ident[:])
                    mm.then_inc(done_pe[kind], 1)
                elif kind == "turn_y":
                    pe.wait_ge(taken["turn_o"], count("turn_o", b, GROUPS - 1))
                    for t in range(QT):
                        mm = pe.transpose(ps[:, t * P:(t + 1) * P], y[:, t, i * P:(i + 1) * P], ident[:])
                    mm.then_inc(done_pe[kind], 1)
                elif kind == "project_o":
                    pe.wait_ge(taken["turn_y"], count("turn_y", b, KC - 1))
                    for s in range(2):
                        t = 2 * i + s
                        for k in range(KC):
                            mm = pe.matmul(ps[:, s * C:(s + 1) * C], yT[:, k, t * P:(t + 1) * P], wo_sb[:, k, :],
                                           start=(k == 0), stop=(k == KC - 1))
                    mm.then_inc(done_pe[kind], 1)

        @block.vector
        def _(dve):
            own = [0]

            def after(instruction):
                own[0] += 1
                instruction.then_inc(s_dve_own, 1)
                dve.wait_ge(s_dve_own, own[0])

            def sum_factors():
                dve.wait_ge(s_vweights, 80)
                for k in range(KC):
                    f = dve.tensor_reduce(wvg_sb[:, k, C:2 * C], fac[:, k].rearrange("p r e -> p e r"),
                                          AX_X, ALU.add)
                f.then_inc(s_factors, 1)

            for step in steps:
                kind, b, i = step
                if kind in WORK_KINDS:
                    ps = work(step)
                if kind == "normalise":
                    dve.wait_ge(s_x[b % X_SLOTS], 16 * (b // X_SLOTS + 1))
                    if b > 0:
                        dve.wait_ge(s_xn, count("normalise", b - 1))
                    for t in range(QT):
                        last = dve.bn_stats(stats[:, t, :], xbuf[:, b % X_SLOTS, t, :])
                    after(last)
                    for t in range(QT):
                        last = dve.bn_aggr(moments[:, t, :], stats[:, t, :])
                    last.then_inc(s_moments, 1)
                    if b == 0:
                        for n in range(2):
                            dve.memset(qk[n][1][DOT_ROWS:ROWS, :, :], 1.0).then_inc(s_ones, 1)
                        dve.memset(vaug[:, :, :, :, HD:HD + 1], 1.0)
                        dve.memset(o_ps[:, :], 0.0).then_inc(s_ones, 1)
                elif kind == "project_qk":
                    n = count(kind, b, i)
                    dve.wait_ge(done_pe[kind], n)
                    if n > 2 and i % 2 == 0:
                        dve.wait_ge(s_rotated, (n - 1) // 2)
                    if b == 0 and i == 0:
                        dve.wait_ge(s_weights, 64)
                    dve.scalar_tensor_tensor(out=by_cos[:, i % 2, :], in0=ps[:, :], scalar=bqk_sb[:, i:i + 1],
                                             in1=cos_t[:], op0=ALU.add, op1=ALU.mult)
                    dve.scalar_tensor_tensor(out=by_sin[:, i % 2, :], in0=ps[:, :], scalar=bqk_sb[:, i:i + 1],
                                             in1=sin_t[:], op0=ALU.add, op1=ALU.mult
                                             ).then_inc(taken[kind], 1)
                elif kind == "project_vg":
                    dve.wait_ge(done_pe[kind], count(kind, b, i))
                    if b >= 2 and i == 0:
                        dve.wait_ge(done_pe["values"], (b - 1) * GROUPS)
                        dve.wait_ge(s_result, count("project_o", b - 2, 1))
                    dve.tensor_tensor(vaug[:, b % 2, i, :, 0:HD],
                                      ps[:, 0:C].rearrange("p (h d) -> p h d", h=H),
                                      bias_sb[:, 0:C].rearrange("p (h d) -> p h d", h=H), ALU.add)
                    dve.scalar_tensor_tensor(out=gate[:, b % 2, i, :], in0=ps[:, C:2 * C],
                                             scalar=float(RANK) ** -0.5, in1=bias_sb[:, C:2 * C],
                                             op0=ALU.mult, op1=ALU.add).then_inc(taken[kind], 1)
                elif kind == "maxima":
                    dve.wait_ge(done_pe[kind], count(kind, b, i))
                    if b > 0 and i == 0:
                        dve.wait_ge(done_pe["shift"], count("shift", b - 1))
                    sps = score_ps[(count(kind, b, i) - 1) % SCORE_BANKS]
                    tile, heads = max_chunk(i // MAX_CHUNKS, i % MAX_CHUNKS)
                    width = (tile + 1) * P
                    dve.tensor_reduce(rowmax[:, tile, heads[0]:heads[0] + len(heads)],
                                      sps[:, 0:len(heads) * width].rearrange("p (h k) -> p h k", k=width),
                                      AX_X, ALU.max).then_inc(taken[kind], 1)
                elif kind == "shift":
                    dve.wait_ge(done_pe[kind], count(kind, b))
                    if b > 0:
                        dve.wait_ge(s_shift[(b - 1) % 2], 16 * SHIFT_ROWS * ((b - 1) // 2 + 1))
                    after(dve.tensor_scalar(shift[:, 0, :], ps[0:H, :], -1.0, None, ALU.mult))
                    dve.scalar_tensor_tensor(out=shift[:, 1, :], in0=ps[0:H, :], scalar=-1.0,
                                             in1=shift[:, 0, :], op0=ALU.mult, op1=ALU.subtract
                                             ).then_inc(taken[kind], 1)
                elif kind == "turn_o":
                    n = count(kind, b, i)
                    dve.wait_ge(done_pe[kind], n)
                    if i == 0 and b > 0:
                        dve.wait_ge(done_pe["turn_y"], count("turn_y", b - 1, KC - 1))
                    o = ps[:, :].rearrange("p (t h d) -> p t h d", t=QT, h=4)
                    after(dve.reciprocal(rden[:], o[:, :, :, HD]))
                    dve.tensor_tensor(y[:, :, 4 * HD * i:4 * HD * (i + 1)].rearrange("p t (h d) -> p t h d", h=4),
                                      o[:, :, :, 0:HD],
                                      rden[:].unsqueeze(3).broadcast_to([P, QT, 4, HD]), ALU.mult
                                      ).then_inc(taken[kind], 1)
                    if n < B * GROUPS:
                        dve.wait_ge(taken[kind], n)
                elif kind == "project_o":
                    dve.wait_ge(done_pe[kind], count(kind, b, i))
                    if b > 0:
                        dve.wait_ge(s_out[i], 16 * b)
                    for s in range(2):
                        r = dve.tensor_tensor(result[:, i, s, :], ps[:, s * C:(s + 1) * C], bias_sb[:, 2 * C:],
                                              ALU.add)
                    r.then_inc(taken[kind], 1)
                if step == ("project_qk", 0, 3):
                    sum_factors()

        @block.scalar
        def _(act):
            for step in steps:
                kind, b, i = step
                if kind in WORK_KINDS:
                    ps = work(step)
                if kind == "turn_x":
                    act.wait_ge(done_pe[kind], count(kind, b, i))
                    if b > 0 and i == 0:
                        act.wait_ge(done_pe["project_qk"], count("project_qk", b - 1, 3))
                        act.wait_ge(done_pe["project_vg"], count("project_vg", b - 1, QT - 1))
                    act.activation(xnT[:, i, :], ps[:, :], ACT.Copy).then_inc(taken[kind], 1)
                elif kind == "high":
                    n = count(kind, b, i)
                    act.wait_ge(s_rotated, n)
                    if b > 0:
                        act.wait_ge(s_stack[(b - 1) % 2][i], 16 * 12 * ((b - 1) // 2 + 1))
                    act.activation(parts[:, i, 0], rotated[:, i], ACT.Copy).then_inc(s_high, 1)
                elif kind == "middle":
                    act.wait_ge(s_rest, count(kind, b, i))
                    act.activation(parts[:, i, 1], rotated[:, i], ACT.Copy).then_inc(s_middle, 1)
                elif kind == "gate_exp":
                    act.wait_ge(taken["project_vg"], count("project_vg", b, QT - 1))
                    if b > 0:
                        act.wait_ge(s_gate, b)
                    act.activation(gate_e[:], gate[:, b % 2], ACT.Tanh, scale=0.5).then_inc(s_gate_e, 1)
                elif kind == "scores":
                    n = count(kind, b, i)
                    act.wait_ge(done_pe[kind], n)
                    pair = b * PAIRS + i // EXP_CHUNKS
                    if b == 0 and i == 0:
                        act.wait_ge(s_factors, 1)
                    if pair >= PROB_SLOTS and i % EXP_CHUNKS == 0:
                        act.wait_ge(done_pe["values"], (pair - PROB_SLOTS) // 2 + 1)
                    act.activation(probs[:, pair % PROB_SLOTS, i % EXP_CHUNKS, :],
                                   exp_ps[(n - 1) % EXP_BANKS][:, :], ACT.Exp, scale=float(HD) ** -0.5
                                   ).then_inc(taken[kind], 1)
                elif kind == "take_o":
                    n = count(kind, b, i)
                    act.wait_ge(done_pe["values"], n)
                    if n > 1:
                        act.wait_ge(done_pe["turn_o"], n - 1)
                    act.activation(oT[:], o_ps[:, :], ACT.Copy).then_inc(taken[kind], 1)
                elif kind == "turn_y":
                    act.wait_ge(done_pe[kind], count(kind, b, i))
                    if b > 0 and i == 0:
                        act.wait_ge(done_pe["project_o"], count("project_o", b - 1, 1))
                    act.activation(yT[:, i, :], ps[:, :], ACT.Copy).then_inc(taken[kind], 1)

        @block.gpsimd
        def _(pool):
            own = [0]

            def after(instruction):
                own[0] += 1
                instruction.then_inc(s_pool_own, 1)
                pool.wait_ge(s_pool_own, own[0])

            after(pool.memset(ident[:], 0.0))
            pool.affine_select(out=ident[:], in_=ident[:], compare_op=ALU.not_equal, fill=1.0, base=0,
                               pattern=[[-1, P]], channel_multiplier=1).then_inc(s_consts, 1)
            pool.wait_ge(s_consts, 1)
            pool.tensor_copy(ident_bf[:], ident[:]).then_inc(s_consts, 1)
            pool.memset(later_k[:], 0.0)
            after(pool.memset(later_q[:], 0.0))
            pool.affine_select(out=later_k[:], in_=later_k[:], compare_op=ALU.is_ge, fill=MASKED, base=0,
                               pattern=[[-1, P]], channel_multiplier=1).then_inc(s_consts, 1)
            pool.affine_select(out=later_q[:], in_=later_q[:], compare_op=ALU.is_ge, fill=MASKED, base=0,
                               pattern=[[1, P]], channel_multiplier=-1).then_inc(s_consts, 1)
            after(pool.memset(minus_half[:], -0.5))
            for kind, b, i in steps:
                if kind == "normalise":
                    pool.wait_ge(s_moments, b + 1)
                    if b > 0:
                        pool.wait_ge(done_pe["turn_x"], count("turn_x", b - 1, KC - 1))
                    after(pool.tensor_scalar(rstd[:], moments[:, :, 1], EPS, None, ALU.add))
                    after(pool.tensor_tensor(rstd[:], rstd[:], minus_half[:], ALU.pow))
                    for t in range(QT):
                        last = pool.tensor_scalar(xn[:, t, :], xbuf[:, b % X_SLOTS, t, :], moments[:, t, 0:1],
                                                  rstd[:, t:t + 1], ALU.subtract, ALU.mult)
                    last.then_inc(s_xn, 1)
                elif kind == "rotate":
                    n = count(kind, b, i)
                    pool.wait_ge(taken["project_qk"], count("project_qk", b, 2 * i + 1))
                    if b > 0:
                        pool.wait_ge(s_low, count("low", b - 1, i))
                        pool.wait_ge(s_middle, count("middle", b - 1, i))
                    pool.tensor_tensor(rotated[:, i, 0, :], by_cos[:, 0, :], by_sin[:, 1, :], ALU.subtract)
                    pool.tensor_tensor(rotated[:, i, 1, :], by_cos[:, 1, :], by_sin[:, 0, :], ALU.add
                                       ).then_inc(s_rotated, 1)
                elif kind == "rest":
                    pool.wait_ge(s_high, count("high", b, i))
                    pool.tensor_tensor(rotated[:, i], rotated[:, i], parts[:, i, 0], ALU.subtract
                                       ).then_inc(s_rest, 1)
                elif kind == "low":
                    pool.wait_ge(s_middle, count("middle", b, i))
                    pool.tensor_tensor(parts[:, i, 2], rotated[:, i], parts[:, i, 1], ALU.subtract
                                       ).then_inc(s_low, 1)
                elif kind == "gate":
                    pool.wait_ge(s_gate_e, b + 1)
                    after(pool.tensor_scalar(gate_e[:], gate_e[:], 0.5, 0.5, ALU.mult, ALU.add))
                    pool.tensor_tensor(gate[:, b % 2], gate[:, b % 2], gate_e[:], ALU.mult
                                       ).then_inc(s_gate, 1)
                elif kind == "project_o":
                    n = count(kind, b, i)
                    pool.wait_ge(taken[kind], n)
                    pool.wait_ge(s_gate, b + 1)
                    pool.tensor_tensor(result[:, i], result[:, i], gate[:, b % 2, 2 * i:2 * i + 2, :],
                                       ALU.mult).then_inc(s_gated, 1)
                    pool.wait_ge(s_gated, n)
                    pool.tensor_tensor(result[:, i], result[:, i], xbuf[:, b % X_SLOTS, 2 * i:2 * i + 2, :],
                                       ALU.add).then_inc(s_result, 1)


def rope_tables():
    p = np.arange(HALF, dtype=np.float32)
    theta = np.power(np.float32(10000.0), -np.float32(2.0) ** p / np.float32(HD)).astype(np.float32)
    pos = np.arange(1, T + 1, dtype=np.float32)
    angle = (np.repeat(theta, H)[:, None] * pos[None, :]).astype(np.float32)
    return np.cos(angle.astype(np.float64)).astype(np.float32), np.sin(angle.astype(np.float64)).astype(np.float32)


def kernel(L0_attn_x, L0_attn_Wqkv, L0_attn_bqkv, L0_attn_Wo, L0_attn_bo, L0_ffn_factors, L0_ffn_bias):
    import concourse.bacc as bacc
    from concourse.bass_utils import run_bass_kernel_spmd as run

    w = np.ascontiguousarray(L0_attn_Wqkv)
    bqkv = np.ascontiguousarray(L0_attn_bqkv)
    order = np.arange(2 * C).reshape(2, H, 2, HALF).transpose(0, 2, 3, 1).reshape(-1)
    cos, sin = rope_tables()
    arrays = {
        "x": np.ascontiguousarray(L0_attn_x),
        "wqk": np.ascontiguousarray(w[order].T),
        "bqk": np.ascontiguousarray(bqkv[order].reshape(4, P).T),
        "wv": np.ascontiguousarray(w[2 * C:].T),
        "wo": np.ascontiguousarray(np.asarray(L0_attn_Wo).T),
        "factors": np.ascontiguousarray(L0_ffn_factors),
        "bias_rows": np.ascontiguousarray(np.broadcast_to(
            np.concatenate([bqkv[2 * C:], np.asarray(L0_ffn_bias), np.asarray(L0_attn_bo)]), (P, 3 * C))),
        "cos": cos,
        "sin": sin,
    }
    nc = bacc.Bacc("TRN2", target_bir_lowering=False, num_devices=1)
    args = [nc.dram_tensor(n, a.shape, mybir.dt.from_np(a.dtype), kind="ExternalInput").ap()
            for n, a in arrays.items()]
    out = nc.dram_tensor("out", (B, T, C), F32, kind="ExternalOutput").ap()
    block_kernel(nc, *args, out)
    return run(nc, [arrays], core_ids=[0]).results[0]["out"]
```

```python
from contextlib import ExitStack

import numpy as np

import concourse.bass as bass
from concourse import mybir

ALU = mybir.AluOpType
ACT = mybir.ActivationFunctionType
AX_X = mybir.AxisListType.X
F32 = mybir.dt.float32
BF16 = mybir.dt.bfloat16

P = 128
B, T, C = 4, 512, 256
H, HD = 16, 16
HALF = HD // 2
RANK = 8
QT = T // P
KC = C // P

Q_PARTS = (0, 0, 1, 1, 0, 2)
K_PARTS = (0, 1, 0, 1, 2, 0)
DOT_ROWS = len(Q_PARTS) * HD
SHIFT_ROWS = 2
ROWS = DOT_ROWS + SHIFT_ROWS

GROUPS = H // 4
PAIRS = H // 2
UNITS = 2
UH = H // UNITS
UR = P // UNITS
UP = PAIRS // UNITS
UG = GROUPS // UNITS
PARITIES = 2
STACK_DMAS = 2 * 2 * len(Q_PARTS)
EPS = 1e-5
MASKED = -1e30
TWO_ONES = float(np.array([0x3F803F80], np.uint32).view(np.float32)[0])

SCORE_BANKS = 3
EXP_BANKS = 2
WORK_BANKS = 2
X_SLOTS = 3
PROB_SLOTS = 4

MAX_CHUNKS = 11
LEAD = 0.5
EXP_CHUNKS = 5


def max_chunk(group, c):
    h = 4 * group
    if c < 4:
        return 3, [h + c]
    if c < 8:
        return 2, [h + c - 4]
    if c < 10:
        return 1, [h + 2 * (c - 8), h + 2 * (c - 8) + 1]
    return 0, [h, h + 1, h + 2, h + 3]


def exp_chunk(pair, c):
    h = 2 * pair
    if c < 2:
        return [(h + c, 0, 0)]
    if c < 4:
        return [(h + c - 2, 1, 0), (h + c - 2, 3, 3 * P)]
    return [(h, 2, 0), (h + 1, 2, 2 * P)]


def prob_place(head, key_tile):
    for c in range(EXP_CHUNKS):
        for h, j, col in exp_chunk(head // 2, c):
            if (h, j) == (head, key_tile):
                return c, col


def timed(steps, start, end):
    return [(start + (end - start) * n / len(steps), step) for n, step in enumerate(steps)]


def attention_steps(b, u):
    s = []
    for pair in range(u * UP, (u + 1) * UP):
        before = (b * PAIRS + pair) // 2 - 1
        gb, g = before // GROUPS, before % GROUPS
        for c in range(EXP_CHUNKS):
            s.append(("scores", b, pair * EXP_CHUNKS + c))
            if pair % 2 == 0 and before >= 0:
                s += {1: [("values", gb, g)], 3: [("take_o", gb, g)]}.get(c, [])
            if pair % 2 == 1 and before >= 0 and c == 0:
                s.append(("turn_o", gb, g))
    return s


def plan():
    steps = []
    for b in range(B):
        at = float(UNITS * b)
        start, span = {0: (-3.2, 0.3), 1: (-1.3, 0.9), 3: (at - 2.8, 0.8)}.get(b, (at - 3.0, 0.8))
        for share, kind, i in (
                (-0.5, "stats", 0), (-0.4, "rstd", 0), (-0.1, "normalise", 0), (0.0, "turn_x", 0), (0.05, "turn_x", 1),
                (0.15, "project_qk", 0), (0.25, "project_qk", 1), (0.3, "rotate", 0), (0.45, "high", 0),
                (0.5, "rest", 0), (0.5, "project_qk", 2), (0.6, "project_qk", 3), (0.65, "middle", 0),
                (0.7, "low", 0), (0.75, "rotate", 1), (0.9, "high", 1), (0.95, "rest", 1),
                (1.1, "middle", 1), (1.15, "low", 1)):
            steps.append((start + span * share, (kind, b, i)))
        steps.append((start - 0.8 * span if b >= X_SLOTS else -9.0, ("load", b, 0)))
        steps += [(start + 1.2 * span, ("stack", b, u)) for u in range(UNITS)]
        start, span = (at - 1.35, 0.45) if b else (-2.0, 0.15)
        steps += timed([("project_vg", b, t) for t in range(QT)] + [("gate_tanh", b, 0), ("gate", b, 0)],
                       start, start + span)
        for u in range(UNITS):
            unit = at + u
            n = UG * MAX_CHUNKS
            steps += timed([("maxima", b, i) for i in range(u * n, (u + 1) * n)], unit - 1.0 - LEAD, unit - LEAD)
            steps.append((unit - LEAD + 0.02, ("shift", b, u)))
            steps += timed(attention_steps(b, u), unit, unit + 1)
        start = at + UNITS + 0.4
        steps += timed([("turn_y", b, 0), ("turn_y", b, 1), ("project_o", b, 0), ("project_o", b, 1)],
                       start, start + 0.2)
    end = UNITS * B
    g = GROUPS - 1
    steps += timed([("values", B - 1, g), ("take_o", B - 1, g), ("turn_o", B - 1, g)], end, end + 0.1)
    return [step for _, step in sorted(steps, key=lambda s: s[0])]


WORK_KINDS = ("turn_x", "project_qk", "project_vg", "shift", "turn_o", "turn_y", "project_o")


def block_kernel(nc, x, wqk, bqk, wv, wo, factors, bias_rows, cos, sin, out):
    steps = plan()
    seen, nth, work_order = {}, {}, []
    for step in steps:
        seen[step[0]] = seen.get(step[0], 0) + 1
        nth[step] = seen[step[0]]
        if step[0] in WORK_KINDS:
            work_order.append(step)
    work_use = {step: n for n, step in enumerate(work_order)}

    def count(kind, b, i=0):
        return nth[(kind, b, i)]

    with ExitStack() as ctx:
        def sb(name, shape, dt=F32):
            return ctx.enter_context(nc.sbuf_tensor(name, shape, dt))

        def bank(name):
            return ctx.enter_context(nc.psum_tensor(name, [P, 512], F32))

        def sem(name):
            return ctx.enter_context(nc.semaphore(name))

        ident = sb("ident", [P, P])
        ident_bf = sb("ident_bf", [P, P], BF16)
        later_k = sb("later_k", [P, P], BF16)
        later_q = sb("later_q", [P, P], BF16)
        cos_t = sb("cos_t", [P, T])
        sin_t = sb("sin_t", [P, T])
        wqk_sb = sb("wqk_sb", [P, KC, 4 * P])
        bqk_sb = sb("bqk_sb", [P, 4])
        wvg_sb = sb("wvg_sb", [P, KC, 2 * C])
        wo_sb = sb("wo_sb", [P, KC, C])
        bias_sb = sb("bias_sb", [P, 3 * C])
        xbuf = sb("xbuf", [P, X_SLOTS, QT, C])
        stats = sb("stats", [P, QT, 6])
        moments = sb("moments", [P, QT, 2])
        rstd = sb("rstd", [P, QT])
        minus_half = sb("minus_half", [P, QT])
        xn = sb("xn", [P, QT, C])
        xnT = sb("xnT", [P, KC, T])
        by_cos = sb("by_cos", [P, 2, T])
        by_sin = sb("by_sin", [P, 2, T])
        rotated = sb("rotated", [P, 2, 2, T])
        parts = sb("parts", [P, 2, 3, 2, T], BF16)
        qk = [[sb(f"stack_{n}{i}", [P, H, T], BF16) for n in "qk"] for i in range(2)]
        vaug = sb("vaug", [P, 2, QT, H, HD + 1])
        gate = sb("gate", [P, 2, QT, C])
        gate_t = sb("gate_t", [P, QT, C])
        rowmax = sb("rowmax", [P, QT, H])
        shift = sb("shift", [UH, SHIFT_ROWS, T], BF16)
        probs = sb("probs", [P, PROB_SLOTS, EXP_CHUNKS, T])
        oT = sb("oT", [P, T])
        rden = sb("rden", [P, QT, 4])
        y = sb("y", [P, QT, C])
        yT = sb("yT", [P, KC, T])
        result = sb("result", [P, 2, 2, C])
        fac = probs[:, 0:2, :, :].rearrange("p a c t -> p (a c t)")[:, 0:KC * RANK * C].rearrange(
            "p (k r e) -> p k r e", k=KC, r=RANK)

        score_ps = [bank(f"score_ps{i}") for i in range(SCORE_BANKS)]
        exp_ps = [bank(f"exp_ps{i}") for i in range(EXP_BANKS)]
        o_ps = bank("o_ps")
        work_ps = [bank(f"work_ps{i}") for i in range(WORK_BANKS)]

        s_weights = sem("weights_loaded")
        s_vweights = sem("vg_weights_loaded")
        s_x = [sem(f"x_loaded{i}") for i in range(X_SLOTS)]
        s_consts = sem("constants_built")
        s_pool_own = sem("pool_own")
        s_dve_own = sem("dve_own")
        s_ones = sem("value_ones_set")
        s_k_ones = sem("stack_ones_set")
        s_factors = sem("factors_summed")
        done_pe = {k: sem(f"pe_{k}") for k in WORK_KINDS + ("maxima", "scores", "values")}
        taken = {k: sem(f"taken_{k}") for k in WORK_KINDS + ("maxima", "scores", "take_o")}
        s_moments = sem("moments_ready")
        s_rstd = sem("rstd_ready")
        s_xn = sem("xn_ready")
        s_rotated = sem("rotated_ready")
        s_high = sem("high_ready")
        s_rest = sem("rest_ready")
        s_middle = sem("middle_ready")
        s_low = sem("low_ready")
        s_stack = [[sem(f"stacked{i}_{u}") for u in range(UNITS)] for i in range(PARITIES)]
        s_shift = [[sem(f"shift_stacked{i}_{u}") for u in range(UNITS)] for i in range(PARITIES)]
        s_gate_t = sem("gate_tanh_ready")
        s_gate = sem("gate_ready")
        s_gated = sem("output_gated")
        s_result = sem("result_ready")
        s_out = [sem(f"out_stored{i}") for i in range(2)]

        x_v = x.rearrange("b (t p) c -> b p t c", p=P)
        out_v = out.rearrange("b (t p) c -> b p t c", p=P)

        def work(step):
            return work_ps[work_use[step] % WORK_BANKS]

        def wait_work_bank(pe, step):
            n = work_use[step] - WORK_BANKS
            if n >= 0:
                before = work_order[n]
                pe.wait_ge(taken[before[0]], nth[before])

        block = ctx.enter_context(nc.Block())

        @block.sync
        def _(sp):
            sp.dma_start(xbuf[:, 0], x_v[0]).then_inc(s_x[0], 16)
            sp.dma_start(wqk_sb[:], wqk.rearrange("(k p) n -> p k n", p=P)).then_inc(s_weights, 16)
            sp.dma_start(bqk_sb[:], bqk).then_inc(s_weights, 16)
            sp.dma_start(cos_t[:], cos).then_inc(s_weights, 16)
            sp.dma_start(sin_t[:], sin).then_inc(s_weights, 16)
            for k in range(KC):
                sp.dma_start(fac[:, k], factors[:, k * P:(k + 1) * P, :].rearrange("r p e -> p r e")
                             ).then_inc(s_vweights, 16)
            sp.dma_start(wvg_sb[:, :, 0:C], wv.rearrange("(k p) n -> p k n", p=P)).then_inc(s_vweights, 16)
            sp.dma_start(bias_sb[:], bias_rows).then_inc(s_vweights, 16)
            sp.dma_start(wo_sb[:], wo.rearrange("(k p) n -> p k n", p=P)).then_inc(s_vweights, 16)
            for kind, b, i in steps:
                if kind == "load" and b > 0:
                    if b >= X_SLOTS:
                        sp.wait_ge(s_result, count("project_o", b - X_SLOTS, 1))
                    sp.dma_start(xbuf[:, b % X_SLOTS], x_v[b]).then_inc(s_x[b % X_SLOTS], 16)
                elif kind == "stack":
                    if b >= PARITIES:
                        sp.wait_ge(done_pe["scores"], count("scores", b - PARITIES, (i + 1) * UP * EXP_CHUNKS - 1))
                    for n, numbers in enumerate((Q_PARTS, K_PARTS)):
                        for part, (kept, signal) in enumerate((("high", s_high), ("middle", s_middle), ("low", s_low))):
                            sp.wait_ge(signal, count(kept, b, n))
                            for g in (g for g, number in enumerate(numbers) if number == part):
                                for half in range(2):
                                    row = g * HD + half * HALF
                                    sp.dma_start(qk[b % PARITIES][n][row:row + HALF, i * UH:(i + 1) * UH, :],
                                                 parts[i * UR:(i + 1) * UR, n, part, half, :]
                                                 ).then_inc(s_stack[b % PARITIES][i], 16)
                elif kind == "project_o":
                    n = count(kind, b, i)
                    sp.wait_ge(s_result, n)
                    sp.dma_start(out_v[b, :, 2 * i:2 * i + 2, :], result[:, i]).then_inc(s_out[i], 16)
            for i in range(2):
                sp.wait_ge(s_out[i], 16 * B)

        @block.tensor
        def _(pe):
            for step in steps:
                kind, b, i = step
                if kind in WORK_KINDS:
                    wait_work_bank(pe, step)
                    ps = work(step)
                if kind == "turn_x":
                    if b == 0 and i == 0:
                        pe.wait_ge(s_consts, 4)
                    pe.wait_ge(s_xn, count("normalise", b))
                    for t in range(QT):
                        mm = pe.transpose(ps[:, t * P:(t + 1) * P], xn[:, t, i * P:(i + 1) * P], ident[:])
                    mm.then_inc(done_pe[kind], 1)
                elif kind == "project_qk":
                    if b == 0 and i == 0:
                        pe.wait_ge(s_weights, 64)
                    pe.wait_ge(taken["turn_x"], count("turn_x", b, KC - 1))
                    for k in range(KC):
                        mm = pe.matmul(ps[:, :], wqk_sb[:, k, i * P:(i + 1) * P], xnT[:, k, :],
                                       start=(k == 0), stop=(k == KC - 1))
                    mm.then_inc(done_pe[kind], 1)
                elif kind == "project_vg":
                    if b == 0 and i == 0:
                        pe.wait_ge(s_vweights, 80)
                        pe.wait_ge(s_factors, 1)
                    for k in range(KC):
                        mm = pe.matmul(ps[:, :], xnT[:, k, i * P:(i + 1) * P], wvg_sb[:, k, :],
                                       start=(k == 0), stop=(k == KC - 1))
                    mm.then_inc(done_pe[kind], 1)
                elif kind == "maxima":
                    n = count(kind, b, i)
                    if n > SCORE_BANKS:
                        pe.wait_ge(taken[kind], n - SCORE_BANKS)
                    if i % (UG * MAX_CHUNKS) == 0:
                        unit = i // (UG * MAX_CHUNKS)
                        pe.wait_ge(s_stack[b % PARITIES][unit], 16 * STACK_DMAS * (b // PARITIES + 1))
                    sps = score_ps[(n - 1) % SCORE_BANKS]
                    tile, heads = max_chunk(i // MAX_CHUNKS, i % MAX_CHUNKS)
                    width = (tile + 1) * P
                    for s, h in enumerate(heads):
                        pe.matmul(sps[:, s * width:(s + 1) * width],
                                  qk[b % 2][0][0:DOT_ROWS, h, tile * P:(tile + 1) * P],
                                  qk[b % 2][1][0:DOT_ROWS, h, 0:width], start=(s == 0), stop=False)
                    diagonal = sps[:, 0:len(heads) * width].rearrange("p (h k) -> p h k", k=width)[:, :, tile * P:]
                    mm = pe.matmul(diagonal, ident_bf[:], later_k[:].unsqueeze(1).broadcast_to([P, len(heads), P]), start=False, stop=True)
                    mm.then_inc(done_pe[kind], 1)
                elif kind == "shift":
                    pe.wait_ge(taken["maxima"], count("maxima", b, (i + 1) * UG * MAX_CHUNKS - 1))
                    for t in range(QT):
                        mm = pe.transpose(ps[0:UH, t * P:(t + 1) * P], rowmax[:, t, i * UH:(i + 1) * UH], ident[:])
                    mm.then_inc(done_pe[kind], 1)
                elif kind == "scores":
                    n = count(kind, b, i)
                    if n > EXP_BANKS:
                        pe.wait_ge(taken[kind], n - EXP_BANKS)
                    if i % (UP * EXP_CHUNKS) == 0:
                        unit = i // (UP * EXP_CHUNKS)
                        pe.wait_ge(s_shift[b % PARITIES][unit], 16 * SHIFT_ROWS * (b // PARITIES + 1))
                        if b == 0 and unit == 0:
                            pe.wait_ge(s_k_ones, PARITIES)
                    eps = exp_ps[(n - 1) % EXP_BANKS]
                    blocks = exp_chunk(i // EXP_CHUNKS, i % EXP_CHUNKS)
                    for n, (h, j, col) in enumerate(blocks):
                        pe.matmul(eps[:, col:col + T - j * P],
                                  qk[b % 2][1][0:ROWS, h, j * P:(j + 1) * P],
                                  qk[b % 2][0][0:ROWS, h, j * P:T], start=(n == 0), stop=False)
                    if len(blocks) == 1:
                        diagonal = eps[:, 0:P]
                    else:
                        step_c = blocks[1][2] // P
                        diagonal = eps[:, :].rearrange("p (n q) -> p n q", q=P)[:, 0:step_c + 1:step_c, :]
                    mm = pe.matmul(diagonal, ident_bf[:], later_q[:].unsqueeze(1).broadcast_to([P, len(blocks), P]), start=False, stop=True)
                    mm.then_inc(done_pe[kind], 1)
                elif kind == "values":
                    pe.wait_ge(taken["scores"], (b * PAIRS + 2 * i + 2) * EXP_CHUNKS)
                    n = count(kind, b, i)
                    if n > 1:
                        pe.wait_ge(taken["take_o"], n - 1)
                    if i == 0:
                        pe.wait_ge(taken["project_vg"], count("project_vg", b, QT - 1))
                        if b == 0:
                            pe.wait_ge(s_ones, 2)
                    for j in range(QT):
                        for s in range(4):
                            h = 4 * i + s
                            c, col = prob_place(h, j)
                            slot = (b * PAIRS + h // 2) % PROB_SLOTS
                            mm = pe.matmul(o_ps[32 * s:32 * s + HD + 1, j * P:T], vaug[:, b % 2, j, h, :],
                                           probs[:, slot, c, col:col + T - j * P],
                                           start=(j == 0), stop=(j == QT - 1))
                    mm.then_inc(done_pe[kind], 1)
                elif kind == "turn_o":
                    pe.wait_ge(taken["take_o"], count("take_o", b, i))
                    for t in range(QT):
                        mm = pe.transpose(ps[:, t * P:(t + 1) * P], oT[:, t * P:(t + 1) * P], ident[:])
                    mm.then_inc(done_pe[kind], 1)
                elif kind == "turn_y":
                    pe.wait_ge(taken["turn_o"], count("turn_o", b, GROUPS - 1))
                    for t in range(QT):
                        mm = pe.transpose(ps[:, t * P:(t + 1) * P], y[:, t, i * P:(i + 1) * P], ident[:])
                    mm.then_inc(done_pe[kind], 1)
                elif kind == "project_o":
                    pe.wait_ge(taken["turn_y"], count("turn_y", b, KC - 1))
                    for s in range(2):
                        t = 2 * i + s
                        for k in range(KC):
                            mm = pe.matmul(ps[:, s * C:(s + 1) * C], yT[:, k, t * P:(t + 1) * P], wo_sb[:, k, :],
                                           start=(k == 0), stop=(k == KC - 1))
                    mm.then_inc(done_pe[kind], 1)

        def rotary_step(eng, kind, b, i):
            if kind == "rotate":
                eng.wait_ge(taken["project_qk"], count("project_qk", b, 2 * i + 1))
                if b > 0:
                    eng.wait_ge(s_low, count("low", b - 1, i))
                    eng.wait_ge(s_middle, count("middle", b - 1, i))
                eng.tensor_tensor(rotated[:, i, 0, :], by_cos[:, 0, :], by_sin[:, 1, :], ALU.subtract)
                eng.tensor_tensor(rotated[:, i, 1, :], by_cos[:, 1, :], by_sin[:, 0, :], ALU.add
                                  ).then_inc(s_rotated, 1)
            elif kind == "rest":
                eng.wait_ge(s_high, count("high", b, i))
                eng.tensor_tensor(rotated[:, i], rotated[:, i], parts[:, i, 0], ALU.subtract
                                  ).then_inc(s_rest, 1)
            else:
                eng.wait_ge(s_middle, count("middle", b, i))
                eng.tensor_tensor(parts[:, i, 2], rotated[:, i], parts[:, i, 1], ALU.subtract
                                  ).then_inc(s_low, 1)

        @block.vector
        def _(dve):
            own = [0]

            def after(instruction):
                own[0] += 1
                instruction.then_inc(s_dve_own, 1)
                dve.wait_ge(s_dve_own, own[0])

            for step in steps:
                kind, b, i = step
                if kind in WORK_KINDS:
                    ps = work(step)
                if kind == "stats":
                    dve.wait_ge(s_x[b % X_SLOTS], 16 * (b // X_SLOTS + 1))
                    for t in range(QT):
                        last = dve.bn_stats(stats[:, t, :], xbuf[:, b % X_SLOTS, t, :])
                    after(last)
                    for t in range(QT):
                        last = dve.bn_aggr(moments[:, t, :], stats[:, t, :])
                    last.then_inc(s_moments, 1)
                elif kind == "normalise":
                    dve.wait_ge(s_rstd, count("rstd", b))
                    if b > 0:
                        dve.wait_ge(done_pe["turn_x"], count("turn_x", b - 1, KC - 1))
                    for t in range(QT):
                        last = dve.tensor_scalar(xn[:, t, :], xbuf[:, b % X_SLOTS, t, :], moments[:, t, 0:1],
                                                 rstd[:, t:t + 1], ALU.subtract, ALU.mult)
                    last.then_inc(s_xn, 1)
                    if b == 0:
                        dve.memset(vaug[:, :, :, :, HD:HD + 1], 1.0).then_inc(s_ones, 1)
                        dve.memset(o_ps[:, :], 0.0).then_inc(s_ones, 1)
                elif kind == "project_qk":
                    n = count(kind, b, i)
                    dve.wait_ge(done_pe[kind], n)
                    if n > 2 and i % 2 == 0:
                        dve.wait_ge(s_rotated, (n - 1) // 2)
                    if b == 0 and i == 0:
                        dve.wait_ge(s_weights, 64)
                    dve.scalar_tensor_tensor(out=by_cos[:, i % 2, :], in0=ps[:, :], scalar=bqk_sb[:, i:i + 1],
                                             in1=cos_t[:], op0=ALU.add, op1=ALU.mult)
                    dve.scalar_tensor_tensor(out=by_sin[:, i % 2, :], in0=ps[:, :], scalar=bqk_sb[:, i:i + 1],
                                             in1=sin_t[:], op0=ALU.add, op1=ALU.mult
                                             ).then_inc(taken[kind], 1)
                elif kind == "project_vg":
                    dve.wait_ge(done_pe[kind], count(kind, b, i))
                    if b >= 2 and i == 0:
                        dve.wait_ge(done_pe["values"], (b - 1) * GROUPS)
                        dve.wait_ge(s_result, count("project_o", b - 2, 1))
                    dve.tensor_tensor(vaug[:, b % 2, i, :, 0:HD],
                                      ps[:, 0:C].rearrange("p (h d) -> p h d", h=H),
                                      bias_sb[:, 0:C].rearrange("p (h d) -> p h d", h=H), ALU.add)
                    dve.scalar_tensor_tensor(out=gate[:, b % 2, i, :], in0=ps[:, C:2 * C],
                                             scalar=float(RANK) ** -0.5, in1=bias_sb[:, C:2 * C],
                                             op0=ALU.mult, op1=ALU.add).then_inc(taken[kind], 1)
                elif kind in ("rotate", "rest", "low") and b == 0:
                    rotary_step(dve, kind, b, i)
                elif kind == "maxima":
                    dve.wait_ge(done_pe[kind], count(kind, b, i))
                    if b > 0 and i % (UG * MAX_CHUNKS) == 0:
                        unit = i // (UG * MAX_CHUNKS)
                        dve.wait_ge(done_pe["shift"], count("shift", b - 1, unit))
                    sps = score_ps[(count(kind, b, i) - 1) % SCORE_BANKS]
                    tile, heads = max_chunk(i // MAX_CHUNKS, i % MAX_CHUNKS)
                    width = (tile + 1) * P
                    dve.tensor_reduce(rowmax[:, tile, heads[0]:heads[0] + len(heads)],
                                      sps[:, 0:len(heads) * width].rearrange("p (h k) -> p h k", k=width),
                                      AX_X, ALU.max).then_inc(taken[kind], 1)
                elif kind == "shift":
                    n = count(kind, b, i)
                    dve.wait_ge(done_pe[kind], n)
                    if n > 1:
                        n -= 2
                        dve.wait_ge(s_shift[n // UNITS % PARITIES][n % UNITS],
                                    16 * SHIFT_ROWS * (n // UNITS // PARITIES + 1))
                    after(dve.tensor_scalar(shift[:, 0, :], ps[0:UH, :], -1.0, None, ALU.mult))
                    dve.scalar_tensor_tensor(out=shift[:, 1, :], in0=ps[0:UH, :], scalar=-1.0,
                                             in1=shift[:, 0, :], op0=ALU.mult, op1=ALU.subtract
                                             ).then_inc(taken[kind], 1)
                elif kind == "turn_o":
                    n = count(kind, b, i)
                    dve.wait_ge(done_pe[kind], n)
                    if i == 0 and b > 0:
                        dve.wait_ge(done_pe["turn_y"], count("turn_y", b - 1, KC - 1))
                    o = ps[:, :].rearrange("p (t h d) -> p t h d", t=QT, h=4)
                    after(dve.reciprocal(rden[:], o[:, :, :, HD]))
                    dve.tensor_tensor(y[:, :, 4 * HD * i:4 * HD * (i + 1)].rearrange("p t (h d) -> p t h d", h=4),
                                      o[:, :, :, 0:HD],
                                      rden[:].unsqueeze(3).broadcast_to([P, QT, 4, HD]), ALU.mult
                                      ).then_inc(taken[kind], 1)
                    if n < B * GROUPS:
                        dve.wait_ge(taken[kind], n)
                elif kind == "project_o":
                    dve.wait_ge(done_pe[kind], count(kind, b, i))
                    if b > 0:
                        dve.wait_ge(s_out[i], 16 * b)
                    for s in range(2):
                        r = dve.tensor_tensor(result[:, i, s, :], ps[:, s * C:(s + 1) * C], bias_sb[:, 2 * C:],
                                              ALU.add)
                    r.then_inc(taken[kind], 1)

        @block.scalar
        def _(act):
            for step in steps:
                kind, b, i = step
                if kind in WORK_KINDS:
                    ps = work(step)
                if kind == "turn_x":
                    act.wait_ge(done_pe[kind], count(kind, b, i))
                    if b > 0 and i == 0:
                        act.wait_ge(done_pe["project_qk"], count("project_qk", b - 1, 3))
                        act.wait_ge(done_pe["project_vg"], count("project_vg", b - 1, QT - 1))
                    act.activation(xnT[:, i, :], ps[:, :], ACT.Copy).then_inc(taken[kind], 1)
                elif kind == "high":
                    n = count(kind, b, i)
                    act.wait_ge(s_rotated, n)
                    if b > 0:
                        for u in range(UNITS):
                            act.wait_ge(s_stack[(b - 1) % PARITIES][u],
                                        16 * STACK_DMAS * ((b - 1) // PARITIES + 1))
                    act.activation(parts[:, i, 0], rotated[:, i], ACT.Copy).then_inc(s_high, 1)
                elif kind == "middle":
                    act.wait_ge(s_rest, count(kind, b, i))
                    act.activation(parts[:, i, 1], rotated[:, i], ACT.Copy).then_inc(s_middle, 1)
                elif kind == "gate_tanh":
                    act.wait_ge(taken["project_vg"], count("project_vg", b, QT - 1))
                    if b > 0:
                        act.wait_ge(s_gate, b)
                    act.activation(gate_t[:], gate[:, b % 2], ACT.Tanh, scale=0.5).then_inc(s_gate_t, 1)
                elif kind == "scores":
                    n = count(kind, b, i)
                    act.wait_ge(done_pe[kind], n)
                    pair = b * PAIRS + i // EXP_CHUNKS
                    if b == 0 and i == 0:
                        act.wait_ge(s_factors, 1)
                    if pair >= PROB_SLOTS and i % EXP_CHUNKS == 0:
                        act.wait_ge(done_pe["values"], (pair - PROB_SLOTS) // 2 + 1)
                    act.activation(probs[:, pair % PROB_SLOTS, i % EXP_CHUNKS, :],
                                   exp_ps[(n - 1) % EXP_BANKS][:, :], ACT.Exp, scale=float(HD) ** -0.5
                                   ).then_inc(taken[kind], 1)
                elif kind == "shift":
                    act.wait_ge(taken["shift"], count("shift", b, i))
                    for r in range(SHIFT_ROWS):
                        act.dma_start(qk[b % PARITIES][0][DOT_ROWS + r:DOT_ROWS + r + 1, i * UH:(i + 1) * UH, :],
                                      shift[:, r, :]).then_inc(s_shift[b % PARITIES][i], 16)
                elif kind == "take_o":
                    n = count(kind, b, i)
                    act.wait_ge(done_pe["values"], n)
                    if n > 1:
                        act.wait_ge(done_pe["turn_o"], n - 1)
                    act.activation(oT[:], o_ps[:, :], ACT.Copy).then_inc(taken[kind], 1)
                elif kind == "turn_y":
                    act.wait_ge(done_pe[kind], count(kind, b, i))
                    if b > 0 and i == 0:
                        act.wait_ge(done_pe["project_o"], count("project_o", b - 1, 1))
                    act.activation(yT[:, i, :], ps[:, :], ACT.Copy).then_inc(taken[kind], 1)

        @block.gpsimd
        def _(pool):
            own = [0]

            def after(instruction):
                own[0] += 1
                instruction.then_inc(s_pool_own, 1)
                pool.wait_ge(s_pool_own, own[0])

            after(pool.memset(ident[:], 0.0))
            pool.affine_select(out=ident[:], in_=ident[:], compare_op=ALU.not_equal, fill=1.0, base=0,
                               pattern=[[-1, P]], channel_multiplier=1).then_inc(s_consts, 1)
            pool.wait_ge(s_consts, 1)
            pool.tensor_copy(ident_bf[:], ident[:]).then_inc(s_consts, 1)
            pool.memset(later_k[:], 0.0)
            after(pool.memset(later_q[:], 0.0))
            pool.affine_select(out=later_k[:], in_=later_k[:], compare_op=ALU.is_ge, fill=MASKED, base=0,
                               pattern=[[-1, P]], channel_multiplier=1).then_inc(s_consts, 1)
            pool.affine_select(out=later_q[:], in_=later_q[:], compare_op=ALU.is_ge, fill=MASKED, base=0,
                               pattern=[[1, P]], channel_multiplier=-1).then_inc(s_consts, 1)
            after(pool.memset(minus_half[:], -0.5))

            def set_up():
                pool.wait_ge(s_vweights, 80)
                half = RANK // 2
                while half > 1:
                    after(pool.tensor_tensor(fac[:, :, 0:half, :], fac[:, :, 0:half, :],
                                             fac[:, :, half:2 * half, :], ALU.add))
                    half //= 2
                pool.tensor_tensor(wvg_sb[:, :, C:2 * C], fac[:, :, 0, :], fac[:, :, 1, :],
                                   ALU.add).then_inc(s_factors, 1)
                pool.wait_ge(s_factors, 1)
                for n in range(PARITIES):
                    pool.memset(qk[n][1][DOT_ROWS:ROWS, :, :].bitcast(F32), TWO_ONES).then_inc(s_k_ones, 1)
                    pool.wait_ge(s_k_ones, n + 1)

            for kind, b, i in steps:
                if kind == "rstd":
                    pool.wait_ge(s_moments, b + 1)
                    if b > 0:
                        pool.wait_ge(s_xn, count("normalise", b - 1))
                    after(pool.tensor_scalar(rstd[:], moments[:, :, 1], EPS, None, ALU.add))
                    pool.tensor_tensor(rstd[:], rstd[:], minus_half[:], ALU.pow).then_inc(s_rstd, 1)
                    if b == 0:
                        set_up()
                elif kind in ("rotate", "rest", "low") and b > 0:
                    rotary_step(pool, kind, b, i)
                elif kind == "gate":
                    pool.wait_ge(s_gate_t, b + 1)
                    after(pool.tensor_scalar(gate_t[:], gate_t[:], 0.5, 0.5, ALU.mult, ALU.add))
                    pool.tensor_tensor(gate[:, b % 2], gate[:, b % 2], gate_t[:], ALU.mult
                                       ).then_inc(s_gate, 1)
                elif kind == "project_o":
                    n = count(kind, b, i)
                    pool.wait_ge(taken[kind], n)
                    pool.wait_ge(s_gate, b + 1)
                    pool.tensor_tensor(result[:, i], result[:, i], gate[:, b % 2, 2 * i:2 * i + 2, :],
                                       ALU.mult).then_inc(s_gated, 1)
                    pool.wait_ge(s_gated, n)
                    pool.tensor_tensor(result[:, i], result[:, i], xbuf[:, b % X_SLOTS, 2 * i:2 * i + 2, :],
                                       ALU.add).then_inc(s_result, 1)


def rope_tables():
    p = np.arange(HALF, dtype=np.float32)
    theta = np.power(np.float32(10000.0), -np.float32(2.0) ** p / np.float32(HD)).astype(np.float32)
    pos = np.arange(1, T + 1, dtype=np.float32)
    angle = (np.tile(np.repeat(theta, UH), UNITS)[:, None] * pos[None, :]).astype(np.float32)
    return np.cos(angle.astype(np.float64)).astype(np.float32), np.sin(angle.astype(np.float64)).astype(np.float32)


def kernel(L0_attn_x, L0_attn_Wqkv, L0_attn_bqkv, L0_attn_Wo, L0_attn_bo, L0_ffn_factors, L0_ffn_bias):
    import concourse.bacc as bacc
    from concourse.bass_utils import run_bass_kernel_spmd as run

    w = np.ascontiguousarray(L0_attn_Wqkv)
    bqkv = np.ascontiguousarray(L0_attn_bqkv)
    order = np.arange(2 * C).reshape(2, UNITS, UH, 2, HALF).transpose(0, 3, 1, 4, 2).reshape(-1)
    cos, sin = rope_tables()
    arrays = {
        "x": np.ascontiguousarray(L0_attn_x),
        "wqk": np.ascontiguousarray(w[order].T),
        "bqk": np.ascontiguousarray(bqkv[order].reshape(4, P).T),
        "wv": np.ascontiguousarray(w[2 * C:].T),
        "wo": np.ascontiguousarray(np.asarray(L0_attn_Wo).T),
        "factors": np.ascontiguousarray(L0_ffn_factors),
        "bias_rows": np.ascontiguousarray(np.broadcast_to(
            np.concatenate([bqkv[2 * C:], np.asarray(L0_ffn_bias), np.asarray(L0_attn_bo)]), (P, 3 * C))),
        "cos": cos,
        "sin": sin,
    }
    nc = bacc.Bacc("TRN2", target_bir_lowering=False, num_devices=1)
    args = [nc.dram_tensor(n, a.shape, mybir.dt.from_np(a.dtype), kind="ExternalInput").ap()
            for n, a in arrays.items()]
    out = nc.dram_tensor("out", (B, T, C), F32, kind="ExternalOutput").ap()
    block_kernel(nc, *args, out)
    return run(nc, [arrays], core_ids=[0]).results[0]["out"]
```

```python
from contextlib import ExitStack

import numpy as np

import concourse.bass as bass
from concourse import mybir

ALU = mybir.AluOpType
ACT = mybir.ActivationFunctionType
AX_X = mybir.AxisListType.X
F32 = mybir.dt.float32
F32R = mybir.dt.float32r
BF16 = mybir.dt.bfloat16

P = 128
B, T, C = 4, 512, 256
H, HD = 16, 16
HALF = HD // 2
RANK = 8
QT = T // P
KC = C // P

Q_PARTS = (0, 0, 1, 1, 0, 2)
K_PARTS = (0, 1, 0, 1, 2, 0)
DOT_ROWS = len(Q_PARTS) * HD
SHIFT_ROWS = 2
ROWS = DOT_ROWS + SHIFT_ROWS

GROUPS = H // 4
PAIRS = H // 2
UNITS = 2
UH = H // UNITS
UR = P // 2
UP = PAIRS // UNITS
UG = GROUPS // UNITS
PARITIES = 2
STACKED_PARTS = (Q_PARTS, K_PARTS)
STACK_DMAS = 2 * 5
FIRST_LOW_DMAS = 2 * 2
EPS = 1e-5
MASKED = -1e30
LOWEST = -3e38
TWO_ONES = float(np.array([0x3F803F80], np.uint32).view(np.float32)[0])

SPLIT_PRODUCTS = ((0, 0), (0, 1), (1, 0))

BANKS = 7
WARM_UP = 12
X_SLOTS = 3
PROB_SLOTS = 3

VECTOR_MASKS_FROM = 1
MAX_CHUNKS = 11
EXP_CHUNKS = 5


def max_chunk(group, c):
    h = 4 * group
    if c < 4:
        return 3, [h + c]
    if c < 8:
        return 2, [h + c - 4]
    if c < 10:
        return 1, [h + 2 * (c - 8), h + 2 * (c - 8) + 1]
    return 0, [h, h + 1, h + 2, h + 3]


def exp_chunk(pair, c):
    h = 2 * pair
    if c < 2:
        return [(h + c, 0, 0)]
    if c < 4:
        return [(h + c - 2, 1, 0), (h + c - 2, 3, 3 * P)]
    return [(h, 2, 0), (h + 1, 2, 2 * P)]


def prob_place(head, key_tile):
    for c in range(EXP_CHUNKS):
        for h, j, col in exp_chunk(head // 2, c):
            if (h, j) == (head, key_tile):
                return c, col


def masked_by_vector(b, heads):
    return len(heads) == 1 or b >= VECTOR_MASKS_FROM


def timed(steps, start, end):
    return [(start + (end - start) * n / len(steps), step) for n, step in enumerate(steps)]


def attention_steps(b, u):
    s = []
    for pair in range(u * UP, (u + 1) * UP):
        before = (b * PAIRS + pair) // 2 - 1
        gb, g = before // GROUPS, before % GROUPS
        for c in range(EXP_CHUNKS):
            s.append(("scores", b, pair * EXP_CHUNKS + c))
            if before >= 0:
                s += [(kind, gb, g) for kind, at in VALUES_AT if at == (pair % 2, c)]
    return s


PROJECT = ((-3.662, 0.02), (-0.717, 1.079), (1.022, 0.935), (3.384, 0.793))
PROJECT_VG = ((-2.624, 0.552), (0.522, 0.039), (2.705, 0.663), (4.663, 0.298))
BIAS_VG = (-1.158, 1.094, 3.177, 4.835)
GATE = (-0.734, 1.336, 3.458, 5.211)
OUTPUT = (2.45, 4.424, 6.549)
END_TURN_Y = 7.536
ATTENTION = ((-0.004, 1), (1, 2.049), (2.049, 3), (3, 4), (4, 5), (5, 6), (6, 6.995), (6.995, 8))
MAXIMA = ((-1.251, -0.533), (-0.483, 0.51), (0.599, 1.599), (1.577, 2.484), (2.496, 3.535), (3.623, 4.456),
          (4.518, 5.48), (5.462, 6.61))
VALUES_AT = (("values", (0, 2)), ("take_o", (0, 2)), ("turn_o", (1, 0)))
CHAIN_FIRST = (("stats", 0, -0.365), ("rstd", 0, -0.15), ("normalise", 0, -0.1), ("turn_x", 0, 0),
               ("turn_x", 1, 0.057), ("project_qk", 0, 0.15), ("project_qk", 1, 0.25), ("rotate", 0, 0.315),
               ("high", 0, 0.377), ("project_qk", 2, 0.342), ("rest", 0, 0.434), ("middle", 0, 0.422),
               ("project_qk", 3, 0.559), ("low", 0, 0.6), ("stack", 0, 0.618), ("rotate", 1, 0.65),
               ("high", 1, 0.7), ("rest", 1, 0.792), ("middle", 1, 0.818), ("low", 1, 0.861),
               ("stack", 1, 0.86), ("split_gate", 0, 0.61))
CHAIN_SECOND = (("stats", 0, -2.7182), ("rstd", 0, -2.7179), ("normalise", 0, -2.7134), ("turn_x", 0, -0.019),
                ("turn_x", 1, 0.051), ("project_qk", 0, 0.181), ("project_qk", 1, 0.191), ("rotate", 0, 0.457),
                ("high", 0, 0.552), ("rest", 0, 0.554), ("middle", 0, 0.65), ("low", 0, 0.644),
                ("stack", 0, 1.113), ("project_qk", 2, 0.658), ("project_qk", 3, 0.666), ("rotate", 1, 0.83),
                ("high", 1, 0.89), ("rest", 1, 0.995), ("middle", 1, 1.158), ("low", 1, 1.15),
                ("stack", 1, 1.207))
CHAIN = (("stats", 0, -0.508), ("rstd", 0, -0.584), ("normalise", 0, -0.459), ("turn_x", 0, -0.019),
         ("turn_x", 1, 0.01), ("project_qk", 0, 0.181), ("project_qk", 1, 0.191), ("rotate", 0, 0.297),
         ("high", 0, 0.46), ("rest", 0, 0.554), ("middle", 0, 0.65), ("low", 0, 0.931), ("stack", 0, 0.859),
         ("project_qk", 2, 0.658), ("project_qk", 3, 0.666), ("rotate", 1, 0.836), ("high", 1, 0.89),
         ("rest", 1, 0.995), ("middle", 1, 1.158), ("low", 1, 1.15), ("stack", 1, 1.36))


def plan():
    steps = []
    for b in range(B):
        start, span = PROJECT[b]
        steps += [(start + span * share, (kind, b, i)) for kind, i, share in (CHAIN_FIRST, CHAIN_SECOND, CHAIN, CHAIN)[b]]
        steps.append((start - 0.8 * span if b >= X_SLOTS else -9.0, ("load", b, 0)))
        start, span = PROJECT_VG[b]
        steps += timed([("project_vg", b, t) for t in range(QT)], start, start + span)
        steps.append((BIAS_VG[b], ("bias_vg", b, 0)))
        steps += [(GATE[b], (kind, b, 0)) for kind in ("gate_tanh", "gate")]
        for u in range(UNITS):
            unit = UNITS * b + u
            n = UG * MAX_CHUNKS
            start, end = MAXIMA[unit]
            steps += timed([("maxima", b, i) for i in range(u * n, (u + 1) * n)], start, end)
            steps.append((end + 0.02, ("shift", b, u)))
            steps += timed(attention_steps(b, u), *ATTENTION[unit])
        if b < B - 1:
            steps += timed([("turn_y", b, 0), ("turn_y", b, 1), ("project_o", b, 0), ("project_o", b, 1)],
                           OUTPUT[b], OUTPUT[b] + 0.2)
    b = B - 1
    steps.append((END_TURN_Y, ("turn_y", b, 0)))
    steps += [(UNITS * B + n, (kind, b, half)) for n, (kind, half) in enumerate((
        ("begin_o", 0), ("begin_o", 1), ("end_values", 0), ("end_values", 1), ("end_take", 0), ("end_take", 1),
        ("end_turn_o", 0), ("end_turn_o", 1), ("end_turn_y", 0), ("end_turn_y", 1),
        ("project_o", 0), ("project_o", 1)))]
    return [step for _, step in sorted(steps, key=lambda s: s[0])]


RING_KINDS = ("turn_x", "project_qk", "project_vg", "maxima", "shift", "scores", "turn_o", "turn_y", "project_o",
              "end_turn_o", "end_turn_y")


def block_kernel(nc, x, wqk, bqk, wv, wo, factors, bias_rows, cos, sin, out):
    steps = plan()
    seen, nth, ring_order = {}, {}, []
    for step in steps:
        seen[step[0]] = seen.get(step[0], 0) + 1
        nth[step] = seen[step[0]]
        if step == ("end_values", B - 1, 1) or (
                step[0] in RING_KINDS and step not in (("project_o", B - 1, 0), ("project_o", B - 1, 1))):
            ring_order.append(step)
        if step[0] == "begin_o":
            ring_order.append(("project_o",) + step[1:])
    ring_place = {step: n for n, step in enumerate(ring_order)}

    def count(kind, b, i=0):
        return nth[(kind, b, i)]

    with ExitStack() as ctx:
        def sb(name, shape, dt=F32):
            return ctx.enter_context(nc.sbuf_tensor(name, shape, dt))

        def bank(name):
            return ctx.enter_context(nc.psum_tensor(name, [P, 512], F32))

        def sem(name):
            return ctx.enter_context(nc.semaphore(name))

        ident = sb("ident", [P, P])
        ident_bf = sb("ident_bf", [P, P], BF16)
        later_k = sb("later_k", [P, T], BF16)
        cos_t = sb("cos_t", [P, T])
        sin_t = sb("sin_t", [P, T])
        wqk_sb = sb("wqk_sb", [P, 2, KC, 4 * P], F32R)
        bqk_sb = sb("bqk_sb", [P, 4])
        wvg_sb = sb("wvg_sb", [P, 2, KC, 2 * C], F32R)
        wo_sb = sb("wo_sb", [P, 2, KC, C], F32R)
        bias_sb = sb("bias_sb", [P, 3 * C])
        xbuf = sb("xbuf", [P, X_SLOTS, QT, C])
        stats = sb("stats", [P, QT, 6])
        moments = sb("moments", [P, QT, 2])
        rstd = sb("rstd", [P, QT])
        minus_half = sb("minus_half", [P, QT])
        xn = sb("xn", [P, QT, C])
        gate_t = xn
        xnT = sb("xnT", [P, 2, KC, T], F32R)
        rotated = [sb(f"rotated{u}", [P, 2, T]) for u in range(UNITS)]
        by_sin = sb("by_sin", [P, 2, T])
        parts = sb("parts", [P, 2, 3, 2, T], BF16)
        qk = [[sb(f"stack_{n}{i}", [P, H, T], BF16) for n in "qk"] for i in range(2)]
        vaug = sb("vaug", [P, 2, QT, H, HD + 1])
        gate = sb("gate", [P, 2, QT, C])
        rowmax = sb("rowmax", [P, QT, H])
        shift = sb("shift", [UH, SHIFT_ROWS, T], BF16)
        probs = sb("probs", [P, PROB_SLOTS, EXP_CHUNKS, T])
        oT = sb("oT", [P, T])
        rden = sb("rden", [P, QT, 4])
        y = sb("y", [P, QT, C])
        yT = sb("yT", [P, 2, KC, T], F32R)
        result = sb("result", [P, 2, 2, C])
        stage = probs[:, :, :, :].rearrange("p a c t -> p (a c t)")
        fac_end = KC * RANK * C
        fac = stage[:, 0:fac_end].rearrange("p (k r e) -> p k r e", k=KC, r=RANK)
        raw_qk = stage[:, fac_end:fac_end + KC * 4 * P].rearrange("p (k n) -> p k n", k=KC)
        raw_v, raw_o = (stage[:, a:a + KC * C].rearrange("p (k n) -> p k n", k=KC)
                        for a in (fac_end + KC * 4 * P, fac_end + KC * (4 * P + C)))

        o_ps = bank("o_ps")
        ring_ps = [bank(f"ring_ps{i}") for i in range(BANKS)]

        s_weights = sem("weights_loaded")
        s_vweights = sem("vg_weights_loaded")
        s_first_x = [sem(f"first_x_loaded{i}") for i in range(2)]
        s_x = [sem(f"x_loaded{i}") for i in range(X_SLOTS)]
        s_consts = sem("constants_built")
        s_pool_own = sem("pool_own")
        s_dve_own = sem("dve_own")
        s_ones = sem("value_ones_set")
        s_k_ones = sem("stack_ones_set")
        s_fac = sem("factors_loaded")
        s_bias = sem("bias_loaded")
        s_factors = sem("factors_summed")
        s_split_high = sem("weights_high")
        s_split = sem("weights_split")
        s_high_x = sem("xnT_high_ready")
        s_high_end = sem("end_yT_high_ready")
        s_high_y = sem("yT_high_ready")
        done_pe = {k: sem(f"pe_{k}") for k in RING_KINDS + ("values", "end_values")}
        taken = {k: sem(f"taken_{k}") for k in RING_KINDS + ("take_o", "end_values")}
        s_moments = sem("moments_ready")
        s_rstd = sem("rstd_ready")
        s_xn = sem("xn_ready")
        s_rotated = sem("rotated_ready")
        s_high = sem("high_ready")
        s_rest = sem("rest_ready")
        s_middle = sem("middle_ready")
        s_low = sem("low_ready")
        s_placed = [sem("high_placed"), sem("middle_placed")]
        s_first_low = sem("first_low_placed")
        s_stack = [[sem(f"stacked{i}_{u}") for u in range(UNITS)] for i in range(PARITIES)]
        s_shift_high = sem("shift_high_ready")
        s_shift = [[sem(f"shift_stacked{i}_{u}") for u in range(UNITS)] for i in range(PARITIES)]
        s_values = sem("values_ready")
        s_gate_z = sem("gate_argument_ready")
        s_gate_t = sem("gate_tanh_ready")
        s_gate = sem("gate_ready")
        s_result = sem("result_ready")
        s_gated = sem("output_gated")
        s_last_result = sem("last_result_ready")
        s_out = [sem(f"out_stored{i}") for i in range(2)]

        x_v = x.rearrange("b (t p) c -> b p t c", p=P)
        out_v = out.rearrange("b (t p) c -> b p t c", p=P)

        def ring_bank(step):
            return ring_ps[ring_place[step] % BANKS]

        def wait_bank(pe, step):
            n = ring_place[step] - BANKS
            if n >= 0:
                before = ring_order[n]
                pe.wait_ge(taken[before[0]], nth[before])

        block = ctx.enter_context(nc.Block())

        def wait_stack(eng, b, u):
            if (b, u) == (0, 0):
                eng.wait_ge(s_first_low, 16 * FIRST_LOW_DMAS)
            in_other_queue = FIRST_LOW_DMAS if (b % PARITIES, u) == (0, 0) else 0
            eng.wait_ge(s_stack[b % PARITIES][u], 16 * (STACK_DMAS * (b // PARITIES + 1) - in_other_queue))

        def place(eng, b, u, n, part):
            kept, signal = (("high", s_high), ("middle", s_middle), ("low", s_low))[part]
            eng.wait_ge(signal, count(kept, b, u))
            row = STACKED_PARTS[n].index(part) * HD
            if part < 2:
                signal_of_place = s_placed[part]
            else:
                signal_of_place = s_stack[b % PARITIES][u] if (b, u) != (0, 0) else s_first_low
            for half in range(2):
                eng.dma_start(qk[b % PARITIES][n][row + half * HALF:row + (half + 1) * HALF,
                                                  u * UH:(u + 1) * UH, :],
                              parts[n * UR:(n + 1) * UR, u, part, half, :]
                              ).then_inc(signal_of_place, 16)

        @block.sync
        def _(sp):
            for half in range(2):
                tiles = slice(half * QT // 2, (half + 1) * QT // 2)
                sp.dma_start(xbuf[:, 0, tiles], x_v[0, :, tiles]).then_inc(s_first_x[half], 16)
            sp.dma_start(raw_qk, wqk.rearrange("(k p) n -> p k n", p=P)).then_inc(s_weights, 16)
            sp.dma_start(bqk_sb[:], bqk).then_inc(s_weights, 16)
            sp.dma_start(cos_t[:], cos).then_inc(s_weights, 16)
            sp.dma_start(sin_t[:], sin).then_inc(s_weights, 16)
            sp.dma_start(raw_v, wv.rearrange("(k p) n -> p k n", p=P)).then_inc(s_vweights, 16)
            sp.dma_start(raw_o, wo.rearrange("(k p) n -> p k n", p=P)).then_inc(s_vweights, 16)
            for k in range(KC):
                sp.dma_start(fac[:, k], factors[:, k * P:(k + 1) * P, :].rearrange("r p e -> p r e")
                             ).then_inc(s_fac, 16)
            sp.dma_start(bias_sb[:], bias_rows).then_inc(s_bias, 16)
            for kind, b, i in steps:
                if kind == "load" and b > 0:
                    if b >= X_SLOTS:
                        sp.wait_ge(s_result, count("project_o", b - X_SLOTS, 1))
                    sp.dma_start(xbuf[:, b % X_SLOTS], x_v[b]).then_inc(s_x[b % X_SLOTS], 16)
                elif kind == "stack":
                    if b >= PARITIES:
                        sp.wait_ge(done_pe["scores"], count("scores", b - PARITIES, (i + 1) * UP * EXP_CHUNKS - 1))
                    stacked = s_stack[b % PARITIES][i]

                    def repeat(n, part):
                        sp.wait_ge(s_placed[part], 4 * 16 * (UNITS * b + i + 1))
                        stack = qk[b % PARITIES][n][:, i * UH:(i + 1) * UH, :]
                        first, *others = (g * HD for g, held in enumerate(STACKED_PARTS[n]) if held == part)
                        for row in others:
                            sp.dma_start(stack[row:row + HD], stack[first:first + HD]).then_inc(stacked, 16)

                    place(sp, b, i, 0, 0)
                    place(sp, b, i, 1, 0)
                    place(sp, b, i, 0, 1)
                    repeat(0, 0)
                    repeat(1, 0)
                    place(sp, b, i, 1, 1)
                    if (b, i) != (0, 0):
                        place(sp, b, i, 0, 2)
                        place(sp, b, i, 1, 2)
                    repeat(0, 1)
                    repeat(1, 1)
                elif kind == "project_o":
                    if b == B - 1:
                        sp.wait_ge(s_last_result, i + 1)
                    else:
                        sp.wait_ge(s_result, count(kind, b, i))
                    sp.dma_start(out_v[b, :, 2 * i:2 * i + 2, :], result[:, i]).then_inc(s_out[i], 16)
            for i in range(2):
                sp.wait_ge(s_out[i], 16 * B)

        products = [(k, parts_of) for k in range(KC) for parts_of in SPLIT_PRODUCTS]

        def end_bank(half):
            return ring_bank(("end_values", B - 1, 1)) if half else o_ps

        def value_products(pe, ps, b, group, start, end):
            for j in range((end - 1) // P + 1):
                first = max(j * P, start)
                for s in range(4):
                    h = 4 * group + s
                    c, col = prob_place(h, j)
                    slot = (b * PAIRS + h // 2) % PROB_SLOTS
                    mm = pe.matmul(ps[32 * s:32 * s + HD + 1, first:end], vaug[:, b % 2, j, h, :],
                                   probs[:, slot, c, col + first - j * P:col + end - j * P],
                                   start=(j == 0), stop=((j + 1) * P >= end))
            return mm

        def output_products(pe, ps, i, some):
            for n, (k, (a, m)) in enumerate(some):
                for s in range(2):
                    t = 2 * i + s
                    mm = pe.matmul(ps[:, s * C:(s + 1) * C], yT[:, a, k, t * P:(t + 1) * P], wo_sb[:, m, k, :],
                                   start=(k == 0 and n == 0 and s == 0), stop=(k == KC - 1 and n == len(some) - 1 and s == 1))
            return mm

        @block.tensor
        def _(pe):
            pe.wait_ge(s_consts, 3)
            for _ in range(WARM_UP):
                pe.matmul(ring_ps[BANKS - 1][:, :], ident_bf[:], later_k[:], start=True, stop=True)
            for step in steps:
                kind, b, i = step
                if kind in RING_KINDS:
                    if step != ("project_o", B - 1, i):
                        wait_bank(pe, step)
                    ps = ring_bank(step)
                if kind == "turn_x":
                    pe.wait_ge(s_xn, count("normalise", b))
                    for t in range(QT):
                        mm = pe.transpose(ps[:, t * P:(t + 1) * P], xn[:, t, i * P:(i + 1) * P], ident[:])
                    mm.then_inc(done_pe[kind], 1)
                elif kind == "project_qk":
                    if b == 0 and i == 0:
                        pe.wait_ge(s_split, 1)
                    pe.wait_ge(taken["turn_x"], count("turn_x", b, KC - 1))
                    for n, (k, (a, m)) in enumerate(products):
                        mm = pe.matmul(ps[:, :], wqk_sb[:, a, k, i * P:(i + 1) * P], xnT[:, m, k, :],
                                       start=(n == 0), stop=(n == len(products) - 1))
                    mm.then_inc(done_pe[kind], 1)
                elif kind == "project_vg":
                    if b == 0 and i == 0:
                        pe.wait_ge(s_split, 4)
                    for n, (k, (a, m)) in enumerate(products):
                        mm = pe.matmul(ps[:, :], xnT[:, a, k, i * P:(i + 1) * P], wvg_sb[:, m, k, :],
                                       start=(n == 0), stop=(n == len(products) - 1))
                    mm.then_inc(done_pe[kind], 1)
                elif kind == "maxima":
                    if i % (UG * MAX_CHUNKS) == 0:
                        unit = i // (UG * MAX_CHUNKS)
                        wait_stack(pe, b, unit)
                    tile, heads = max_chunk(i // MAX_CHUNKS, i % MAX_CHUNKS)
                    width = (tile + 1) * P
                    for s, h in enumerate(heads):
                        mm = pe.matmul(ps[:, s * width:(s + 1) * width],
                                       qk[b % 2][0][0:DOT_ROWS, h, tile * P:(tile + 1) * P],
                                       qk[b % 2][1][0:DOT_ROWS, h, 0:width],
                                       start=(s == 0),
                                       stop=(s == len(heads) - 1 and masked_by_vector(b, heads)))
                    if not masked_by_vector(b, heads):
                        diagonal = ps[:, 0:len(heads) * width].rearrange("p (h k) -> p h k", k=width)[:, :, tile * P:]
                        later = later_k[:, T - P:].unsqueeze(1).broadcast_to([P, len(heads), P])
                        mm = pe.matmul(diagonal, ident_bf[:], later, start=False, stop=True)
                    mm.then_inc(done_pe[kind], 1)
                elif kind == "shift":
                    pe.wait_ge(taken["maxima"], count("maxima", b, (i + 1) * UG * MAX_CHUNKS - 1))
                    for t in range(QT):
                        mm = pe.transpose(ps[0:UH, t * P:(t + 1) * P], rowmax[:, t, i * UH:(i + 1) * UH], ident[:])
                    mm.then_inc(done_pe[kind], 1)
                elif kind == "scores":
                    if i % (UP * EXP_CHUNKS) == 0:
                        unit = i // (UP * EXP_CHUNKS)
                        pe.wait_ge(s_shift[b % PARITIES][unit], 16 * SHIFT_ROWS * (b // PARITIES + 1))
                        if b == 0 and unit == 0:
                            pe.wait_ge(s_k_ones, PARITIES)
                    blocks = exp_chunk(i // EXP_CHUNKS, i % EXP_CHUNKS)
                    for n, (h, j, col) in enumerate(blocks):
                        pe.matmul(ps[:, col:col + T - j * P],
                                  qk[b % 2][1][0:ROWS, h, j * P:(j + 1) * P],
                                  qk[b % 2][0][0:ROWS, h, j * P:T], start=(n == 0), stop=False)
                    if len(blocks) == 1:
                        diagonal = ps[:, 0:P]
                    else:
                        step_c = blocks[1][2] // P
                        diagonal = ps[:, :].rearrange("p (n q) -> p n q", q=P)[:, 0:step_c + 1:step_c, :]
                    own = ident_bf[:].unsqueeze(1).broadcast_to([P, len(blocks), P])
                    mm = pe.matmul(diagonal, later_k[:, T - P:], own, start=False, stop=True)
                    mm.then_inc(done_pe[kind], 1)
                elif kind == "values":
                    pe.wait_ge(taken["scores"], (b * PAIRS + 2 * i + 2) * EXP_CHUNKS)
                    n = count(kind, b, i)
                    if n > 1:
                        pe.wait_ge(taken["take_o"], n - 1)
                    if i == 0:
                        pe.wait_ge(s_values, b + 1)
                        if b == 0:
                            pe.wait_ge(s_ones, 2)
                    value_products(pe, o_ps, b, i, 0, T).then_inc(done_pe[kind], 1)
                elif kind == "end_values":
                    if i == 0:
                        pe.wait_ge(taken["scores"], B * PAIRS * EXP_CHUNKS)
                        pe.wait_ge(taken["take_o"], B * GROUPS - 1)
                    else:
                        wait_bank(pe, step)
                    value_products(pe, end_bank(i), b, GROUPS - 1, i * T // 2, (i + 1) * T // 2
                                   ).then_inc(done_pe[kind], 1)
                elif kind == "end_turn_o":
                    pe.wait_ge(taken["end_values"], i + 1)
                    for t in range(i * QT // 2, (i + 1) * QT // 2):
                        mm = pe.transpose(ps[:, t * P:(t + 1) * P], oT[:, t * P:(t + 1) * P], ident[:])
                    mm.then_inc(done_pe[kind], 1)
                elif kind == "end_turn_y":
                    pe.wait_ge(taken["end_turn_o"], i + 1)
                    for t in range(i * QT // 2, (i + 1) * QT // 2):
                        mm = pe.transpose(ps[:, t * P:(t + 1) * P], y[:, t, C - P:], ident[:])
                    mm.then_inc(done_pe[kind], 1)
                elif kind == "turn_o":
                    pe.wait_ge(taken["take_o"], count("take_o", b, i))
                    for t in range(QT):
                        mm = pe.transpose(ps[:, t * P:(t + 1) * P], oT[:, t * P:(t + 1) * P], ident[:])
                    mm.then_inc(done_pe[kind], 1)
                elif kind == "turn_y":
                    pe.wait_ge(taken["turn_o"], count("turn_o", b, (i + 1) * GROUPS // KC - 1))
                    for t in range(QT):
                        mm = pe.transpose(ps[:, t * P:(t + 1) * P], y[:, t, i * P:(i + 1) * P], ident[:])
                    mm.then_inc(done_pe[kind], 1)
                elif kind == "begin_o":
                    wait_bank(pe, ("project_o", b, i))
                    pe.wait_ge(taken["turn_y"], count("turn_y", b, 0))
                    output_products(pe, ring_bank(("project_o", b, i)), i, products[:len(SPLIT_PRODUCTS)])
                elif kind == "project_o":
                    if b < B - 1:
                        pe.wait_ge(taken["turn_y"], count("turn_y", b, KC - 1))
                    else:
                        pe.wait_ge(taken["end_turn_y"], i + 1)
                    rest = products[len(SPLIT_PRODUCTS):] if b == B - 1 else products
                    output_products(pe, ps, i, rest).then_inc(done_pe[kind], 1)

        weight_splits = [(raw_qk, wqk_sb[:]), (raw_v, wvg_sb[:, :, :, 0:C]), (raw_o, wo_sb[:]),
                         (fac[:, :, 0, :], wvg_sb[:, :, :, C:])]

        def rotary_step(eng, kind, b, i):
            if kind == "rotate":
                eng.wait_ge(taken["project_qk"], count("project_qk", b, 2 * i + 1))
                eng.tensor_tensor(rotated[i][:, 0, :], rotated[i][:, 0, :], by_sin[:, 1, :], ALU.subtract)
                eng.tensor_tensor(rotated[i][:, 1, :], rotated[i][:, 1, :], by_sin[:, 0, :], ALU.add
                                  ).then_inc(s_rotated, 1)
            elif kind == "rest":
                eng.wait_ge(s_high, count("high", b, i))
                eng.tensor_tensor(rotated[i][:], rotated[i][:], parts[:, i, 0], ALU.subtract
                                  ).then_inc(s_rest, 1)
            else:
                eng.wait_ge(s_middle, count("middle", b, i))
                eng.tensor_tensor(parts[:, i, 2], rotated[i][:], parts[:, i, 1], ALU.subtract
                                  ).then_inc(s_low, 1)

        def normalise(eng, b):
            eng.wait_ge(s_rstd, count("rstd", b))
            if b > 0:
                eng.wait_ge(done_pe["turn_x"], count("turn_x", b - 1, KC - 1))
                if b > 1:
                    eng.wait_ge(s_gate, b - 1)
            for t in range(QT):
                last = eng.tensor_scalar(xn[:, t, :], xbuf[:, b % X_SLOTS, t, :], moments[:, t, 0:1],
                                         rstd[:, t:t + 1], ALU.subtract, ALU.mult)
            last.then_inc(s_xn, 1)

        @block.vector
        def _(dve):
            own = [0]

            def after(instruction):
                own[0] += 1
                instruction.then_inc(s_dve_own, 1)
                dve.wait_ge(s_dve_own, own[0])

            def split_low(n):
                raw, split = weight_splits[n]
                dve.wait_ge(s_split_high, n + 1)
                dve.tensor_tensor(split[:, 1], raw, split[:, 0].bitcast(F32), ALU.subtract).then_inc(s_split, 1)

            for step in steps:
                kind, b, i = step
                if kind in RING_KINDS:
                    ps = ring_bank(step)
                if kind == "turn_x":
                    dve.wait_ge(s_high_x, count(kind, b, i))
                    dve.tensor_tensor(xnT[:, 1, i, :], ps[:, :], xnT[:, 0, i, :].bitcast(F32), ALU.subtract
                                      ).then_inc(taken[kind], 1)
                    if b == 0 and i == KC - 1:
                        split_low(1)
                        split_low(2)
                        dve.memset(o_ps[:, :], 0.0).then_inc(s_ones, 1)
                elif kind == "turn_y":
                    dve.wait_ge(s_high_y, count(kind, b, i))
                    dve.tensor_tensor(yT[:, 1, i, :], ps[:, :], yT[:, 0, i, :].bitcast(F32), ALU.subtract
                                      ).then_inc(taken[kind], 1)
                elif kind == "end_turn_o":
                    dve.wait_ge(done_pe[kind], i + 1)
                    tiles = slice(i * QT // 2, (i + 1) * QT // 2)
                    o = ps[:, :].rearrange("p (t h d) -> p t h d", t=QT, h=4)[:, tiles]
                    after(dve.reciprocal(rden[:, tiles], o[:, :, :, HD]))
                    dve.tensor_tensor(y[:, tiles, C - 4 * HD:].rearrange("p t (h d) -> p t h d", h=4),
                                      o[:, :, :, 0:HD],
                                      rden[:, tiles].unsqueeze(3).broadcast_to([P, QT // 2, 4, HD]), ALU.mult
                                      ).then_inc(taken[kind], 1)
                elif kind == "end_turn_y":
                    dve.wait_ge(s_high_end, i + 1)
                    half = slice(i * T // 2, (i + 1) * T // 2)
                    dve.tensor_tensor(yT[:, 1, KC - 1, half], ps[:, half], yT[:, 0, KC - 1, half].bitcast(F32),
                                      ALU.subtract).then_inc(taken[kind], 1)
                if kind == "stats":
                    if b > 0:
                        dve.wait_ge(s_x[b % X_SLOTS], 16 * (b // X_SLOTS + (b % X_SLOTS > 0)))
                    for t in range(QT):
                        if b == 0 and t % 2 == 0:
                            dve.wait_ge(s_first_x[t // 2], 16)
                        last = dve.bn_stats(stats[:, t, :], xbuf[:, b % X_SLOTS, t, :])
                    after(last)
                    if b > 0:
                        dve.wait_ge(s_xn, b)
                    for t in range(QT):
                        last = dve.bn_aggr(moments[:, t, :], stats[:, t, :])
                    last.then_inc(s_moments, 1)
                elif kind == "normalise":
                    normalise(dve, b)
                    if b > 0:
                        continue
                    dve.memset(vaug[:, :, :, :, HD:HD + 1], 1.0).then_inc(s_ones, 1)
                    split_low(0)
                elif kind == "split_gate":
                    split_low(3)
                elif kind == "project_qk":
                    n = count(kind, b, i)
                    dve.wait_ge(done_pe[kind], n)
                    if n > 2 and i % 2 == 0:
                        dve.wait_ge(s_rotated, n // 2)
                    if b > 0 and i % 2 == 0:
                        dve.wait_ge(s_low, count("low", b - 1, i // 2))
                    dve.scalar_tensor_tensor(out=rotated[i // 2][:, i % 2, :], in0=ps[:, :], scalar=bqk_sb[:, i:i + 1],
                                             in1=cos_t[:], op0=ALU.add, op1=ALU.mult)
                    dve.scalar_tensor_tensor(out=by_sin[:, i % 2, :], in0=ps[:, :], scalar=bqk_sb[:, i:i + 1],
                                             in1=sin_t[:], op0=ALU.add, op1=ALU.mult
                                             ).then_inc(taken[kind], 1)
                elif kind in ("rotate", "rest", "low") and b == 0:
                    rotary_step(dve, kind, b, i)
                elif kind == "maxima":
                    dve.wait_ge(done_pe[kind], count(kind, b, i))
                    if b == 0 and i == 0:
                        dve.wait_ge(s_consts, 3)
                    if b > 0 and i % (UG * MAX_CHUNKS) == 0:
                        unit = i // (UG * MAX_CHUNKS)
                        dve.wait_ge(done_pe["shift"], count("shift", b - 1, unit))
                    tile, heads = max_chunk(i // MAX_CHUNKS, i % MAX_CHUNKS)
                    width = (tile + 1) * P
                    if masked_by_vector(b, heads):
                        for s, h in enumerate(heads):
                            scores = ps[:, s * width:(s + 1) * width]
                            last = dve.tensor_tensor_reduce(scores, scores, later_k[:, T - width:], 1.0, LOWEST,
                                                            ALU.add, ALU.max, rowmax[:, tile, h:h + 1])
                    else:
                        last = dve.tensor_reduce(rowmax[:, tile, heads[0]:heads[0] + len(heads)],
                                                 ps[:, 0:len(heads) * width].rearrange("p (h k) -> p h k", k=width),
                                                 AX_X, ALU.max)
                    last.then_inc(taken[kind], 1)
                elif kind == "shift":
                    dve.wait_ge(s_shift_high, count(kind, b, i))
                    dve.scalar_tensor_tensor(out=shift[:, 1, :], in0=ps[0:UH, :], scalar=-1.0,
                                             in1=shift[:, 0, :], op0=ALU.mult, op1=ALU.subtract
                                             ).then_inc(taken[kind], 1)
                elif kind == "turn_o":
                    n = count(kind, b, i)
                    dve.wait_ge(done_pe[kind], n)
                    if i == 0 and b > 0:
                        dve.wait_ge(done_pe["turn_y"], count("turn_y", b - 1, KC - 1))
                    o = ps[:, :].rearrange("p (t h d) -> p t h d", t=QT, h=4)
                    after(dve.reciprocal(rden[:], o[:, :, :, HD]))
                    dve.tensor_tensor(y[:, :, 4 * HD * i:4 * HD * (i + 1)].rearrange("p t (h d) -> p t h d", h=4),
                                      o[:, :, :, 0:HD],
                                      rden[:].unsqueeze(3).broadcast_to([P, QT, 4, HD]), ALU.mult
                                      ).then_inc(taken[kind], 1)
                    if n < B * GROUPS:
                        dve.wait_ge(taken[kind], n)
                elif kind == "project_o":
                    n = count(kind, b, i)
                    dve.wait_ge(done_pe[kind], n)
                    if b > 0:
                        dve.wait_ge(s_out[i], 16 * b)
                    out_ps = ps[:, :].rearrange("p (t c) -> p t c", c=C)
                    if b < B - 1:
                        bias_o = bias_sb[:, 2 * C:].unsqueeze(1).broadcast_to([P, 2, C])
                        dve.tensor_tensor(result[:, i], out_ps, bias_o, ALU.add).then_inc(taken[kind], 1)
                    else:
                        dve.wait_ge(s_gate, b + 1)
                        tiles = slice(2 * i, 2 * i + 2)
                        dve.tensor_tensor(result[:, i], out_ps, gate[:, b % 2, tiles, :], ALU.mult
                                          ).then_inc(taken[kind], 1)
                        dve.wait_ge(taken[kind], n)
                        dve.tensor_tensor(result[:, i], result[:, i], xbuf[:, b % X_SLOTS, tiles, :], ALU.add
                                          ).then_inc(s_last_result, 1)

        @block.scalar
        def _(act):
            def split_high(n):
                raw, split = weight_splits[n]
                act.activation(split[:, 0], raw, ACT.Copy).then_inc(s_split_high, 1)

            act.wait_ge(s_weights, 64)
            split_high(0)
            for step in steps:
                kind, b, i = step
                if kind in RING_KINDS:
                    ps = ring_bank(step)
                if kind == "turn_x":
                    act.wait_ge(done_pe[kind], count(kind, b, i))
                    if b > 0 and i == 0:
                        act.wait_ge(done_pe["project_qk"], count("project_qk", b - 1, 3))
                        act.wait_ge(done_pe["project_vg"], count("project_vg", b - 1, QT - 1))
                    act.activation(xnT[:, 0, i, :], ps[:, :], ACT.Copy).then_inc(s_high_x, 1)
                    if b == 0 and i == KC - 1:
                        act.wait_ge(s_vweights, 32)
                        split_high(1)
                        split_high(2)
                elif kind == "high":
                    n = count(kind, b, i)
                    act.wait_ge(s_rotated, n)
                    if b > 0:
                        wait_stack(act, b - 1, i)
                    act.activation(parts[:, i, 0], rotated[i][:], ACT.Copy).then_inc(s_high, 1)
                elif kind == "split_gate":
                    act.wait_ge(s_factors, 1)
                    split_high(3)
                elif kind == "middle":
                    act.wait_ge(s_rest, count(kind, b, i))
                    act.activation(parts[:, i, 1], rotated[i][:], ACT.Copy).then_inc(s_middle, 1)
                elif kind == "project_vg":
                    act.wait_ge(done_pe[kind], count(kind, b, i))
                    if b >= 2 and i == 0:
                        act.wait_ge(done_pe["values"], (b - 1) * GROUPS)
                        act.wait_ge(s_result, count("project_o", b - 2, 1))
                    act.activation(vaug[:, b % 2, i, :, 0:HD], ps[:, 0:C].rearrange("p (h d) -> p h d", h=H), ACT.Copy)
                    act.activation(gate[:, b % 2, i, :], ps[:, C:2 * C], ACT.Copy, scale=float(RANK) ** -0.5
                                   ).then_inc(taken[kind], 1)
                elif kind == "gate_tanh":
                    act.wait_ge(s_gate_z, b + 1)
                    act.wait_ge(done_pe["turn_x"], count("turn_x", min(b + 1, B - 1), KC - 1))
                    act.activation(gate_t[:], gate[:, b % 2], ACT.Tanh, scale=0.5).then_inc(s_gate_t, 1)
                elif kind == "scores":
                    n = count(kind, b, i)
                    act.wait_ge(done_pe[kind], n)
                    pair = b * PAIRS + i // EXP_CHUNKS
                    if b == 0 and i == 0:
                        act.wait_ge(s_split, 4)
                    if pair >= PROB_SLOTS and i % EXP_CHUNKS == 0:
                        act.wait_ge(done_pe["values"], (pair - PROB_SLOTS) // 2 + 1)
                    act.activation(probs[:, pair % PROB_SLOTS, i % EXP_CHUNKS, :],
                                   ps[:, :], ACT.Exp, scale=float(HD) ** -0.5
                                   ).then_inc(taken[kind], 1)
                elif kind == "shift":
                    n = count(kind, b, i)
                    act.wait_ge(done_pe[kind], n)
                    if n > 1:
                        old_b, old_unit = divmod(n - 2, UNITS)
                        act.wait_ge(s_shift[old_b % PARITIES][old_unit],
                                    16 * SHIFT_ROWS * (old_b // PARITIES + 1))
                    act.activation(shift[:, 0, :], ps[0:UH, :], ACT.Copy, scale=-1.0).then_inc(s_shift_high, 1)
                    act.wait_ge(taken["shift"], n)
                    for r in range(SHIFT_ROWS):
                        act.dma_start(qk[b % PARITIES][0][DOT_ROWS + r:DOT_ROWS + r + 1, i * UH:(i + 1) * UH, :],
                                      shift[:, r, :]).then_inc(s_shift[b % PARITIES][i], 16)
                elif kind == "take_o":
                    n = count(kind, b, i)
                    act.wait_ge(done_pe["values"], n)
                    if n > 1:
                        act.wait_ge(done_pe["turn_o"], n - 1)
                    act.activation(oT[:], o_ps[:, :], ACT.Copy).then_inc(taken[kind], 1)
                elif kind == "end_take":
                    act.wait_ge(done_pe["end_values"], i + 1)
                    if i == 0:
                        act.wait_ge(done_pe["turn_o"], B * GROUPS - 1)
                    half = slice(i * T // 2, (i + 1) * T // 2)
                    act.activation(oT[:, half], end_bank(i)[:, half], ACT.Copy).then_inc(taken["end_values"], 1)
                elif kind == "end_turn_y":
                    act.wait_ge(done_pe[kind], i + 1)
                    half = slice(i * T // 2, (i + 1) * T // 2)
                    act.activation(yT[:, 0, KC - 1, half], ps[:, half], ACT.Copy).then_inc(s_high_end, 1)
                elif kind == "turn_y":
                    act.wait_ge(done_pe[kind], count(kind, b, i))
                    if b > 0 and i == 0:
                        act.wait_ge(done_pe["project_o"], count("project_o", b - 1, 1))
                    act.activation(yT[:, 0, i, :], ps[:, :], ACT.Copy).then_inc(s_high_y, 1)

        @block.gpsimd
        def _(pool):
            own = [0]

            def after(instruction):
                own[0] += 1
                instruction.then_inc(s_pool_own, 1)
                pool.wait_ge(s_pool_own, own[0])

            after(pool.memset(ident[:], 0.0))
            pool.affine_select(out=ident[:], in_=ident[:], compare_op=ALU.not_equal, fill=1.0, base=0,
                               pattern=[[-1, P]], channel_multiplier=1).then_inc(s_consts, 1)
            pool.wait_ge(s_consts, 1)
            pool.tensor_copy(ident_bf[:], ident[:]).then_inc(s_consts, 1)
            after(pool.memset(later_k[:], 0.0))
            pool.affine_select(out=later_k[:, T - P:], in_=later_k[:, T - P:], compare_op=ALU.is_ge, fill=MASKED,
                               base=0, pattern=[[-1, P]], channel_multiplier=1).then_inc(s_consts, 1)
            after(pool.memset(minus_half[:], -0.5))

            def set_up():
                pool.wait_ge(s_fac, 16 * KC)
                half = RANK // 2
                while half > 1:
                    after(pool.tensor_tensor(fac[:, :, 0:half, :], fac[:, :, 0:half, :],
                                             fac[:, :, half:2 * half, :], ALU.add))
                    half //= 2
                pool.tensor_tensor(fac[:, :, 0, :], fac[:, :, 0, :], fac[:, :, 1, :],
                                   ALU.add).then_inc(s_factors, 1)

            def set_ones():
                pool.wait_ge(s_factors, 1)
                before = steps[:steps.index(("bias_vg", 0, 0))]
                pool.wait_ge(s_rstd, sum(step[0] == "rstd" for step in before))
                for n in range(PARITIES):
                    pool.memset(qk[n][1][DOT_ROWS:ROWS, :, :].bitcast(F32), TWO_ONES).then_inc(s_k_ones, 1)
                    pool.wait_ge(s_k_ones, n + 1)

            for kind, b, i in steps:
                if kind == "rstd":
                    pool.wait_ge(s_moments, b + 1)
                    if b > 0:
                        pool.wait_ge(s_xn, count("normalise", b - 1))
                    after(pool.tensor_scalar(rstd[:], moments[:, :, 1], EPS, None, ALU.add))
                    pool.tensor_tensor(rstd[:], rstd[:], minus_half[:], ALU.pow).then_inc(s_rstd, 1)
                    if b == 0:
                        set_up()
                elif kind in ("rotate", "rest", "low") and b > 0:
                    rotary_step(pool, kind, b, i)
                elif kind == "stack" and (b, i) == (0, 0):
                    place(pool, b, i, 0, 2)
                    place(pool, b, i, 1, 2)
                elif kind == "bias_vg":
                    if b == 0:
                        set_ones()
                        pool.wait_ge(s_bias, 16)
                    pool.wait_ge(taken["project_vg"], count("project_vg", b, QT - 1))
                    for h in range(2):
                        heads = slice(h * H // 2, (h + 1) * H // 2)
                        bias_v = bias_sb[:, 0:C].rearrange("p (h d) -> p h d", h=H)[:, heads]
                        v = vaug[:, b % 2, :, heads, 0:HD]
                        last = pool.tensor_tensor(v, v, bias_v.unsqueeze(1).broadcast_to([P, QT, H // 2, HD]), ALU.add)
                    last.then_inc(s_values, 1)
                    bias_g = bias_sb[:, C:2 * C].unsqueeze(1).broadcast_to([P, QT, C])
                    pool.tensor_tensor(gate[:, b % 2], gate[:, b % 2], bias_g, ALU.add).then_inc(s_gate_z, 1)
                elif kind == "gate":
                    pool.wait_ge(s_gate_t, b + 1)
                    after(pool.tensor_scalar(gate_t[:], gate_t[:], 0.5, 0.5, ALU.mult, ALU.add))
                    silu = pool.tensor_tensor(gate[:, b % 2], gate[:, b % 2], gate_t[:], ALU.mult)
                    if b == B - 1:
                        after(silu)
                        bias_o = bias_sb[:, 2 * C:].unsqueeze(1).broadcast_to([P, QT, C])
                        after(pool.tensor_tensor(gate_t[:], gate[:, b % 2], bias_o, ALU.mult))
                        x_b = xbuf[:, b % X_SLOTS]
                        silu = pool.tensor_tensor(x_b, x_b, gate_t[:], ALU.add)
                    silu.then_inc(s_gate, 1)
                elif kind == "project_o" and b < B - 1:
                    n = count(kind, b, i)
                    pool.wait_ge(taken[kind], n)
                    pool.tensor_tensor(result[:, i], result[:, i], gate[:, b % 2, 2 * i:2 * i + 2, :], ALU.mult
                                       ).then_inc(s_gated, 1)
                    pool.wait_ge(s_gated, n)
                    pool.tensor_tensor(result[:, i], result[:, i], xbuf[:, b % X_SLOTS, 2 * i:2 * i + 2, :], ALU.add
                                       ).then_inc(s_result, 1)


def rope_tables():
    p = np.arange(HALF, dtype=np.float32)
    theta = np.power(np.float32(10000.0), -np.float32(2.0) ** p / np.float32(HD)).astype(np.float32)
    pos = np.arange(1, T + 1, dtype=np.float32)
    angle = (np.tile(np.repeat(theta, UH), 2)[:, None] * pos[None, :]).astype(np.float32)
    return np.cos(angle.astype(np.float64)).astype(np.float32), np.sin(angle.astype(np.float64)).astype(np.float32)


def kernel(L0_attn_x, L0_attn_Wqkv, L0_attn_bqkv, L0_attn_Wo, L0_attn_bo, L0_ffn_factors, L0_ffn_bias):
    import concourse.bacc as bacc
    from concourse.bass_utils import run_bass_kernel_spmd as run

    w = np.ascontiguousarray(L0_attn_Wqkv)
    bqkv = np.ascontiguousarray(L0_attn_bqkv)
    order = np.arange(2 * C).reshape(2, UNITS, UH, 2, HALF).transpose(1, 3, 0, 4, 2).reshape(-1)
    cos, sin = rope_tables()
    arrays = {
        "x": np.ascontiguousarray(L0_attn_x),
        "wqk": np.ascontiguousarray(w[order].T),
        "bqk": np.ascontiguousarray(bqkv[order].reshape(4, P).T),
        "wv": np.ascontiguousarray(w[2 * C:].T),
        "wo": np.ascontiguousarray(np.asarray(L0_attn_Wo).T),
        "factors": np.ascontiguousarray(L0_ffn_factors),
        "bias_rows": np.ascontiguousarray(np.broadcast_to(
            np.concatenate([bqkv[2 * C:], np.asarray(L0_ffn_bias), np.asarray(L0_attn_bo)]), (P, 3 * C))),
        "cos": cos,
        "sin": sin,
    }
    nc = bacc.Bacc("TRN2", target_bir_lowering=False, num_devices=1)
    args = [nc.dram_tensor(n, a.shape, mybir.dt.from_np(a.dtype), kind="ExternalInput").ap()
            for n, a in arrays.items()]
    out = nc.dram_tensor("out", (B, T, C), F32, kind="ExternalOutput").ap()
    block_kernel(nc, *args, out)
    return run(nc, [arrays], core_ids=[0]).results[0]["out"]
```
